# Optimizing a Trainium2 kernel written in Bass

```python
import numpy as np
import jax
import jax.numpy as jnp

def _softmax(x, axis=-1):
    return jax.nn.softmax(x, axis=axis)

def _gelu(x):
    return jax.nn.gelu(x, approximate=True)

def _silu(x):
    return jax.nn.silu(x)

def _sigmoid(x):
    return jax.nn.sigmoid(x)

def _layernorm(x, axis=-1, eps=1e-05):
    m = jnp.mean(x, axis=axis, keepdims=True)
    v = jnp.var(x, axis=axis, keepdims=True)
    return (x - m) / jnp.sqrt(v + eps)

def _scatter_add(tgt, idx, src, axis=0):
    return tgt.at[idx].add(src)

def _segment_sum(src, seg, n):
    return jax.ops.segment_sum(src, seg, n)
kernel_name = 'mk_gnn_preln_d4_gnn_r8_81ebe8'

def setup_inputs(seed: int=0):
    np.random.seed(seed)
    _w = jnp.asarray

    def _rec_inputs():
        import jax
        import jax.numpy as jnp
        _gk = jax.random.key(seed)
        x = -0.000202 + 1 * jax.random.normal(jax.random.fold_in(_gk, 1), (12500, 64), jnp.float32)
        _s = jax.random.randint(jax.random.fold_in(_gk, 2), (100000,), 0, 12500, jnp.int32)
        _d = jax.random.randint(jax.random.fold_in(_gk, 3), (100000,), 0, 12500, jnp.int32)
        _loop = jnp.arange(12500, dtype=jnp.int32)
        src = jnp.concatenate([_s, _d, _loop])
        dst = jnp.concatenate([_d, _s, _loop])
        _o = jnp.argsort(dst, stable=True)
        src = src[_o]
        dst = dst[_o]
        edge_attr_64 = -5.16925e-05 + 1.00005 * jax.random.normal(jax.random.fold_in(_gk, 13), (212500, 64), jnp.float32)
        edge_weight = jax.random.uniform(jax.random.fold_in(_gk, 15), (212500,), jnp.float32, 0.0, 1)
        return (x, src, dst, edge_attr_64, edge_weight)
    x, src, dst, edge_attr_64, edge_weight = _rec_inputs()

    def _L0_gnn_setup():
        import jax, jax.numpy as jnp
        import numpy as np
        N = 12500
        E = 200000
        IN_F = 64
        OUT_F = 64
        BN_EPS = 1e-05

        def _t_o_inv_perm(n):
            idx = np.arange(n)
            p = idx * 4 % n + idx * 4 // n
            inv = np.empty(n, dtype=np.int64)
            inv[p] = idx
            return (p, inv)

        def make_hamilton(weight):
            r, i, j, k = jnp.split(weight, 4, axis=1)
            hamilton = jnp.concatenate([jnp.concatenate([r, -i, -j, -k], axis=1), jnp.concatenate([i, r, -k, j], axis=1), jnp.concatenate([j, k, r, -i], axis=1), jnp.concatenate([k, -j, i, r], axis=1)], axis=0)
            return hamilton
        key = jax.random.key(seed)
        ks = jax.random.split(key, 5)
        x = jax.random.normal(ks[0], (N, IN_F), dtype=jnp.float32)
        edge_row = jax.random.randint(ks[1], (E,), 0, N, dtype=jnp.int64)
        edge_col = jax.random.randint(ks[2], (E,), 0, N, dtype=jnp.int64)
        edge_val = jax.random.uniform(ks[3], (E,), dtype=jnp.float32)
        stdv = np.sqrt(6.0 / (IN_F // 4 + OUT_F))
        weight = jax.random.uniform(ks[4], (IN_F // 4, OUT_F), minval=-stdv, maxval=stdv, dtype=jnp.float32)
        gamma = jnp.ones((OUT_F,), dtype=jnp.float32)
        beta = jnp.zeros((OUT_F,), dtype=jnp.float32)
        return {'x': x, 'edge_row': edge_row, 'edge_col': edge_col, 'edge_val': edge_val, 'weight': weight, 'gamma': gamma, 'beta': beta}
    _L0_gnn_all = _L0_gnn_setup()
    _L0_gnn_in = {k: v for k, v in _L0_gnn_all.items() if k in ('weight', 'gamma', 'beta')}
    del _L0_gnn_all

    def _L1_gnn_setup():
        import jax, jax.numpy as jnp
        import numpy as np
        N_NODES = 12500
        N_EDGES = 156250
        D_IN = 64
        D_OUT = 64
        key = jax.random.key(seed)
        k1, k2, k3, k4 = jax.random.split(key, 4)
        features = jax.random.normal(k1, (N_NODES, D_IN), dtype=jnp.float32)
        limit = float(np.sqrt(6.0 / (D_IN + D_OUT)))
        weight = jax.random.uniform(k2, (D_IN, D_OUT), minval=-limit, maxval=limit, dtype=jnp.float32)
        bias = jnp.zeros((D_OUT,), dtype=jnp.float32)
        src = jax.random.randint(k3, (N_EDGES,), 0, N_NODES, dtype=jnp.int32)
        dst = jax.random.randint(k4, (N_EDGES,), 0, N_NODES, dtype=jnp.int32)
        return {'features': features, 'weight': weight, 'bias': bias, 'src': src, 'dst': dst, 'n_nodes': N_NODES}
    _L1_gnn_all = _L1_gnn_setup()
    _L1_gnn_in = {k: v for k, v in _L1_gnn_all.items() if k in ('weight', 'bias')}
    del _L1_gnn_all

    def _L2_gnn_setup():
        import jax, jax.numpy as jnp
        import numpy as np
        N_NODES = 12500
        N_EDGES = 200000
        D = 64
        key = jax.random.key(seed)
        ks = jax.random.split(key, 7)
        x = jax.random.normal(ks[0], (N_NODES, D), dtype=jnp.float32)
        edge_index = jax.random.randint(ks[1], (2, N_EDGES), 0, N_NODES, dtype=jnp.int64)
        edge_attr = jax.random.normal(ks[2], (N_EDGES, D), dtype=jnp.float32)
        s = 1.0 / np.sqrt(D)
        W1 = jax.random.normal(ks[3], (D, D), dtype=jnp.float32) * s
        b1 = jnp.zeros((D,), dtype=jnp.float32)
        W2 = jax.random.normal(ks[4], (D, D), dtype=jnp.float32) * s
        b2 = jnp.zeros((D,), dtype=jnp.float32)
        return {'x': x, 'edge_index': edge_index, 'edge_attr': edge_attr, 'W1': W1, 'b1': b1, 'W2': W2, 'b2': b2}
    _L2_gnn_all = _L2_gnn_setup()
    _L2_gnn_in = {k: v for k, v in _L2_gnn_all.items() if k in ('W1', 'b1', 'W2', 'b2')}
    del _L2_gnn_all

    def _L3_gnn_setup():
        import jax, jax.numpy as jnp
        import numpy as np
        EPS = 1e-05

        def _bn(h, g, b):
            m = h.mean(axis=0)
            v = ((h - m) ** 2).mean(axis=0)
            return (h - m) * jax.lax.rsqrt(v + EPS) * g + b
        key = jax.random.key(seed)
        ks = jax.random.split(key, 12)
        N, E, G = (6250, 100000, 16)
        Dn = De = Du = Dout = 64
        x = jax.random.normal(ks[0], (N, Dn), jnp.float32)
        edge_index = jax.random.randint(ks[1], (2, E), 0, N, jnp.int64)
        edge_attr = jax.random.normal(ks[2], (E, De), jnp.float32)
        u = jax.random.normal(ks[3], (G, Du), jnp.float32)
        batch = jnp.sort(jax.random.randint(ks[4], (N,), 0, G, jnp.int64))
        s = lambda k, i, o: jax.random.normal(k, (i, o), jnp.float32) * (1.0 / np.sqrt(i))
        return {'x': x, 'edge_index': edge_index, 'edge_attr': edge_attr, 'u': u, 'batch': batch, 'W1a': s(ks[5], Dn + De, Dout), 'g1a': jnp.ones((Dout,)), 'b1a': jnp.zeros((Dout,)), 'W1b': s(ks[6], Dout, Dout), 'g1b': jnp.ones((Dout,)), 'b1b': jnp.zeros((Dout,)), 'W2a': s(ks[7], Dn + Dout + Du, Dout), 'g2a': jnp.ones((Dout,)), 'b2a': jnp.zeros((Dout,)), 'W2b': s(ks[8], Dout, Dout), 'g2b': jnp.ones((Dout,)), 'b2b': jnp.zeros((Dout,))}
    _L3_gnn_all = _L3_gnn_setup()
    _L3_gnn_in = {k: v for k, v in _L3_gnn_all.items() if k in ('u', 'W1a', 'g1a', 'b1a', 'W1b', 'g1b', 'b1b', 'W2a', 'g2a', 'b2a', 'W2b', 'g2b', 'b2b')}
    del _L3_gnn_all
    return {'x': x, 'src': src, 'dst': dst, 'edge_attr_64': edge_attr_64, 'edge_weight': edge_weight, 'L0_gnn_weight': _L0_gnn_in['weight'], 'L0_gnn_gamma': _L0_gnn_in['gamma'], 'L0_gnn_beta': _L0_gnn_in['beta'], 'L1_gnn_weight': _L1_gnn_in['weight'], 'L1_gnn_bias': _L1_gnn_in['bias'], 'L2_gnn_W1': _L2_gnn_in['W1'], 'L2_gnn_b1': _L2_gnn_in['b1'], 'L2_gnn_W2': _L2_gnn_in['W2'], 'L2_gnn_b2': _L2_gnn_in['b2'], 'L3_gnn_u': _L3_gnn_in['u'], 'L3_gnn_W1a': _L3_gnn_in['W1a'], 'L3_gnn_g1a': _L3_gnn_in['g1a'], 'L3_gnn_b1a': _L3_gnn_in['b1a'], 'L3_gnn_W1b': _L3_gnn_in['W1b'], 'L3_gnn_g1b': _L3_gnn_in['g1b'], 'L3_gnn_b1b': _L3_gnn_in['b1b'], 'L3_gnn_W2a': _L3_gnn_in['W2a'], 'L3_gnn_g2a': _L3_gnn_in['g2a'], 'L3_gnn_b2a': _L3_gnn_in['b2a'], 'L3_gnn_W2b': _L3_gnn_in['W2b'], 'L3_gnn_g2b': _L3_gnn_in['g2b'], 'L3_gnn_b2b': _L3_gnn_in['b2b']}

def reference(x, src, dst, edge_attr_64, edge_weight, L0_gnn_weight, L0_gnn_gamma, L0_gnn_beta, L1_gnn_weight, L1_gnn_bias, L2_gnn_W1, L2_gnn_b1, L2_gnn_W2, L2_gnn_b2, L3_gnn_u, L3_gnn_W1a, L3_gnn_g1a, L3_gnn_b1a, L3_gnn_W1b, L3_gnn_g1b, L3_gnn_b1b, L3_gnn_W2a, L3_gnn_g2a, L3_gnn_b2a, L3_gnn_W2b, L3_gnn_g2b, L3_gnn_b2b):
    import jax
    import jax.numpy as jnp

    def _L0_gnn_ref(x, edge_row, edge_col, edge_val, weight, gamma, beta):
        import jax, jax.numpy as jnp
        import numpy as np
        N = 12500
        E = 200000
        IN_F = 64
        OUT_F = 64
        BN_EPS = 1e-05

        def _t_o_inv_perm(n):
            idx = np.arange(n)
            p = idx * 4 % n + idx * 4 // n
            inv = np.empty(n, dtype=np.int64)
            inv[p] = idx
            return (p, inv)

        def make_hamilton(weight):
            r, i, j, k = jnp.split(weight, 4, axis=1)
            hamilton = jnp.concatenate([jnp.concatenate([r, -i, -j, -k], axis=1), jnp.concatenate([i, r, -k, j], axis=1), jnp.concatenate([j, k, r, -i], axis=1), jnp.concatenate([k, -j, i, r], axis=1)], axis=0)
            return hamilton
        n_in = x.shape[1]
        n_out = weight.shape[1]
        hamilton = make_hamilton(weight)
        _, inv_in = _t_o_inv_perm(n_in)
        _, inv_out = _t_o_inv_perm(n_out)
        hamilton = hamilton[inv_in][:, inv_out]
        support = x @ hamilton
        msg = edge_val[:, None] * support[edge_col]
        out = jax.ops.segment_sum(msg, edge_row, num_segments=x.shape[0])
        mean = jnp.mean(out, axis=0)
        var = jnp.mean((out - mean) ** 2, axis=0)
        y = gamma * (out - mean) * jax.lax.rsqrt(var + BN_EPS) + beta
        return jnp.tanh(y)

    def _L1_gnn_ref(features, weight, bias, src, dst, n_nodes):
        import jax, jax.numpy as jnp
        import numpy as np
        N_NODES = 12500
        N_EDGES = 156250
        D_IN = 64
        D_OUT = 64
        ones_e = jnp.ones(src.shape[0], dtype=features.dtype)
        deg_out = jnp.maximum(jax.ops.segment_sum(ones_e, src, num_segments=n_nodes), 1.0)
        deg_in = jnp.maximum(jax.ops.segment_sum(ones_e, dst, num_segments=n_nodes), 1.0)
        h = features * (deg_out ** (-0.5))[:, None] @ weight
        rst = jax.ops.segment_sum(h[src], dst, num_segments=n_nodes)
        rst = rst * (deg_in ** (-0.5))[:, None] + bias
        return rst

    def _L2_gnn_ref(x, edge_index, edge_attr, W1, b1, W2, b2):
        import jax, jax.numpy as jnp
        import numpy as np
        N_NODES = 12500
        N_EDGES = 200000
        D = 64
        src = edge_index[0]
        dst = edge_index[1]
        msg = jax.nn.relu(x[src] + edge_attr)
        agg = jax.ops.segment_sum(msg, dst, num_segments=x.shape[0])
        h = x + agg
        h = jax.nn.relu(h @ W1 + b1)
        return h @ W2 + b2

    def _L3_gnn_ref(x, edge_index, edge_attr, u, batch, W1a, g1a, b1a, W1b, g1b, b1b, W2a, g2a, b2a, W2b, g2b, b2b):
        import jax, jax.numpy as jnp
        import numpy as np
        EPS = 1e-05

        def _bn(h, g, b):
            m = h.mean(axis=0)
            v = ((h - m) ** 2).mean(axis=0)
            return (h - m) * jax.lax.rsqrt(v + EPS) * g + b
        N = x.shape[0]
        row, col = (edge_index[0], edge_index[1])
        h = jnp.concatenate([x[col], edge_attr], axis=1)
        h = jax.nn.relu(_bn(h @ W1a, g1a, b1a))
        h = _bn(h @ W1b, g1b, b1b)
        seg = jax.ops.segment_sum(h, row, num_segments=N)
        cnt = jax.ops.segment_sum(jnp.ones((h.shape[0],), h.dtype), row, num_segments=N)
        agg = seg / jnp.maximum(cnt, 1.0)[:, None]
        h2 = jnp.concatenate([x, agg, u[batch]], axis=1)
        h2 = jax.nn.relu(_bn(h2 @ W2a, g2a, b2a))
        return _bn(h2 @ W2b, g2b, b2b)
    edge_index = jnp.stack([src, dst])
    batch0 = jnp.zeros((12500,), jnp.int32)
    h = jnp.maximum(_layernorm(x, axis=-1), 0.0)
    x = x + _L0_gnn_ref(h, src, dst, edge_weight, L0_gnn_weight, L0_gnn_gamma, L0_gnn_beta)
    h = jnp.maximum(_layernorm(x, axis=-1), 0.0)
    x = x + _L1_gnn_ref(h, L1_gnn_weight, L1_gnn_bias, src, dst, 12500)
    h = jnp.maximum(_layernorm(x, axis=-1), 0.0)
    x = x + _L2_gnn_ref(h, edge_index, edge_attr_64, L2_gnn_W1, L2_gnn_b1, L2_gnn_W2, L2_gnn_b2)
    h = jnp.maximum(_layernorm(x, axis=-1), 0.0)
    x = x + _L3_gnn_ref(h, edge_index, edge_attr_64, L3_gnn_u, batch0, L3_gnn_W1a, L3_gnn_g1a, L3_gnn_b1a, L3_gnn_W1b, L3_gnn_g1b, L3_gnn_b1b, L3_gnn_W2a, L3_gnn_g2a, L3_gnn_b2a, L3_gnn_W2b, L3_gnn_g2b, L3_gnn_b2b)
    return x

_drawn_inputs = setup_inputs


def setup_inputs(seed=0):
    import zlib

    import numpy as np

    out = dict(_drawn_inputs(seed))
    spreads = {'L0_gnn_gamma': (1.0, 0.6),
     'L0_gnn_beta': (0.0, 0.1),
     'L1_gnn_bias': (0.0, 0.1),
     'L2_gnn_b1': (0.0, 0.8),
     'L2_gnn_b2': (0.0, 0.718),
     'L3_gnn_g1a': (1.0, 0.6),
     'L3_gnn_b1a': (0.0, 0.8),
     'L3_gnn_g1b': (1.0, 0.6),
     'L3_gnn_b1b': (0.0, 0.8),
     'L3_gnn_g2a': (1.0, 0.6),
     'L3_gnn_b2a': (0.0, 0.8),
     'L3_gnn_g2b': (1.0, 0.6),
     'L3_gnn_b2b': (0.0, 0.753)}
    factors = {'L3_gnn_u': 8.0}
    for name, (base, spread) in spreads.items():
        noise = np.random.default_rng([zlib.crc32(name.encode()), seed]).standard_normal(out[name].shape)
        drawn = base * np.exp(spread * noise) if base else spread * noise
        out[name] = jnp.asarray(drawn.astype(out[name].dtype))
    for name, factor in factors.items():
        out[name] = (out[name] * factor).astype(out[name].dtype)
    return out
```

```python
from contextlib import ExitStack

import concourse.bass as bass
from concourse import mybir

F32 = mybir.dt.float32
I32 = mybir.dt.int32
I16 = mybir.dt.int16
ALU = mybir.AluOpType
ACT = mybir.ActivationFunctionType
AX = mybir.AxisListType.X
ENG = mybir.EngineType

P = 128
N = 12500
E = 212500
D = 64
NB = -(-N // P)
NP = NB * P
LAST = N - (NB - 1) * P
NT = -(-E // P)
TC = -(-NT // P)
EP = TC * P * P
PAD_SOURCE = NP - 1
U = 32
K = -(-(NT + NB - 1) // U) * U
IT = K // U
KC = -(-K // P)
PAD_TARGET = (K - NT + 1) * P
RW = D + 1
REP = 8
ACC_ROWS = NP + P
Q = NB // 2
GP = 7
GROUPS = Q // GP
EPS = 1e-5
CLEARS = 3
CLEAR = ACC_ROWS // P // CLEARS * RW
CLEAR_AT = NB * RW - CLEAR
assert ACC_ROWS // P % CLEARS == 0 and CLEAR_AT >= 2 * NT - 1
SLOTS = 8
RUNS = U // SLOTS


WEIGHTS = ("hamilton", "l1", "l2a", "l2b", "l3_h", "l3_b", "l3_x", "l3_agg", "l3_out")
VECTORS = ("gamma", "beta", "l2_b1", "l2_b2", "l3_u", "g2a", "b2a", "g2b", "b2b", "scale", "shift")


ROWS = ("l1_bias", "g1a", "b1a", "g1b", "b1b")


class Memory:
    pass


SERIAL = []


def new_semaphore(nc, name):
    SERIAL.append(name)
    return nc.alloc_semaphore(name=f"{name}_{len(SERIAL)}")


def sems(nc, *names):
    return {n: new_semaphore(nc, n) for n in names}


def ring(nc, name, n):
    return [new_semaphore(nc, f"{name}{i}_") for i in range(n)]


def node_rows(ap, lo, hi):
    return ap[lo * P:hi * P, :].rearrange("(b p) f -> p b f", p=P)


def allocate(nc, ctx):
    def sb(name, shape, dt=F32):
        return ctx.enter_context(nc.sbuf_tensor(name, shape, dt))

    def dram(name, shape, dt=F32):
        return nc.dram_tensor(name, shape, dt).ap()

    m = Memory()
    m.x = sb("x_nodes", [P, NB, D])
    m.h = sb("h_nodes", [P, NB, RW])
    m.both = sb("pair_nodes", [P, 2 * NB * RW])
    m.pair = m.both[:, 0:NB * 2 * D].rearrange("p (b f) -> p b f", b=NB)
    m.work = sb("work_nodes", [P, NB * RW])
    m.cols = sb("step_cols", [P, 4, K])
    m.src, m.rel, m.wt, m.member = (m.cols[:, i, :] for i in range(4))
    m.gather_idx = sb("gather_idx", [P, K + U], I32)
    m.scatter_idx = sb("scatter_idx", [P, K], I32)
    m.block_of = sb("block_of_step", [1, K], I32)
    m.gram = sb("gram", [D, RW])
    m.turned_gram = sb("turned_gram", [P, RW])
    m.scale_row, m.shift_row = sb("scale_row", [P, 2 * D]), sb("shift_row", [P, 2 * D])
    m.row = {n: sb(f"row_{n}", [P, D]) for n in ROWS}
    m.valid, m.twice, m.u0 = sb("valid", [P, 1]), sb("twice", [P, 1]), sb("u0", [D, 1])
    m.share, m.count = sb("share", [P, 1]), sb("count", [P, 1])
    m.rows = sb("step_rows", [P, 2, SLOTS, 2, P], I16)
    compared = sb("compared", [P, 8, P])
    m.compared = compared[:, :, :].rearrange("p q n -> p (q n)")
    m.onehot, m.same = compared[:, 0:4, :], compared[:, 4:8, :]
    m.together = compared[:, 0:GP, :].rearrange("p q n -> p (q n)")
    m.turned = m.rows[:, :, :, :, :].rearrange("p h s r e -> p (h s r e)").bitcast(F32)[:, 0:GP * P]
    m.slot = [sb(f"slot{i}", [P, RW + 1 + D]) for i in range(SLOTS)]
    m.hidden_in = [m.gather_idx[:, i * SLOTS * D:(i + 1) * SLOTS * D].bitcast(F32) for i in range(2)]
    m.msg = sb("message", [P, 4, 2 * D])
    m.msg_junk = sb("junk", [P, 2, P])
    m.attr_turned = m.rows[:, :, :, :, :].rearrange("p h s r e -> p (h s r e)").bitcast(F32)[0:D, 0:SLOTS * P]
    m.hidden_out = [m.msg[:, :, :].rearrange("p r f -> p (r f)"), m.same.rearrange("p q n -> p (q n)")]
    m.zero = sb("zero", [P, RW])
    m.idx = [sb(f"idx{i}", [P, SLOTS], I32) for i in range(RUNS)]
    m.ident = sb("ident", [P, P])
    m.before = sb("before", [P, P])
    m.ones = sb("ones", [P, P])
    m.fold = sb("fold_halves", [P, P])
    m.iota_row = sb("iota_row", [P, P])
    m.part = sb("partition_no", [P, 1])
    m.trash = sb("trash_row", [P, 1])
    m.dout = sb("degree_out", [P, NB])
    m.din = sb("degree_in", [P, NB])
    m.small = sb("small", [P, 6 * D])
    m.stat = sb("stat", [P, NB])
    m.stat2 = sb("stat2", [P, NB])
    m.w = {n: sb(f"w_{n}", [P, P]) for n in WEIGHTS}
    m.w1a, m.w1a_ea = sb("w1a", [P, D]), sb("w1a_attr", [D, D])
    m.col = {n: sb(f"col_{n}", [P, 1]) for n in VECTORS}
    m.repeats = sb("repeats", [P, U])
    m.psum = [ctx.enter_context(nc.psum_tensor(f"psum{i}", [P, 512], F32)) for i in range(8)]
    m.hidden = dram("attr_products", (K // SLOTS * P, SLOTS * D))
    m.tile_keys = dram("tile_keys", (TC * P,))
    m.step_tile, m.step_block = dram("step_tile", (KC * P,), I32), dram("step_block", (KC * P,), I32)
    m.step_rows = dram("step_row_keys", (KC * P, 2 * P), I16)
    m.table = dram("node_table", (NP, D))
    m.acc = [dram(f"by_source{i}", (ACC_ROWS, RW)) for i in range(REP)]
    return m


def constants_and_nodes(nc, m, a):
    with ExitStack() as ctx:
        s = sems(nc, "iotas", "zeros_ready", "loaded", "blank")
        block = ctx.enter_context(nc.Block())

        @block.gpsimd
        def _(pool):
            g = nc.gpsimd
            g.iota(m.iota_row[:, :], pattern=[[1, P]], base=0, channel_multiplier=0,
                   allow_small_or_imprecise_dtypes=True)
            g.iota(m.part[:, :], pattern=[[0, 1]], base=0, channel_multiplier=1,
                   allow_small_or_imprecise_dtypes=True)
            g.iota(m.trash[:, :], pattern=[[0, 1]], base=NP, channel_multiplier=1,
                   allow_small_or_imprecise_dtypes=True)
            pool.wait_ge(s["blank"], 4)
            g.affine_select(out=m.ident[:, :], in_=m.ident[:, :], compare_op=ALU.not_equal, fill=1.0,
                            base=0, pattern=[[-1, P]], channel_multiplier=1)
            g.affine_select(out=m.before[:, :], in_=m.ones[:, :], compare_op=ALU.is_gt, fill=0.0,
                            base=0, pattern=[[-1, P]], channel_multiplier=1)
            for shift in (-D, 0, D):
                part = g.affine_select(out=m.fold[:, :], in_=m.fold[:, :], compare_op=ALU.not_equal, fill=1.0,
                                       base=shift, pattern=[[-1, P]], channel_multiplier=1)
                part.then_inc(s["iotas"], 1)
                pool.wait_ge(s["iotas"], (shift + D) // D + 1)

        @block.vector
        def _(dve):
            v = nc.vector
            v.memset(m.ident[:, :], 0.0).then_inc(s["blank"], 1)
            v.memset(m.ones[:, :], 1.0).then_inc(s["blank"], 1)
            v.memset(m.fold[:, :], 0.0).then_inc(s["blank"], 1)
            v.memset(m.x[:, NB - 1, :], 0.0).then_inc(s["blank"], 1)
            v.memset(m.work[:, CLEAR_AT:CLEAR_AT + CLEAR], 0.0).then_inc(s["zeros_ready"], 1)
            v.memset(m.h[:, :, D:RW], 1.0)

        @block.sync
        def _(sp):
            sp.dma_start(m.x[:, 0:NB - 1, :], node_rows(a["x"], 0, NB - 1)).then_inc(s["loaded"], 16)
            sp.wait_ge(s["blank"], 4)
            sp.dma_start(m.x[0:LAST, NB - 1, :], a["x"][(NB - 1) * P:N, :]).then_inc(s["loaded"], 16)
            sp.wait_ge(s["zeros_ready"], 1)
            for acc in m.acc:
                rows = acc.rearrange("(p r) f -> p (r f)", p=P)
                for lo in range(0, ACC_ROWS // P * RW, CLEAR):
                    sp.dma_start(rows[:, lo:lo + CLEAR], m.work[:, CLEAR_AT:CLEAR_AT + CLEAR]).then_inc(m.cleared, 16)
            sp.wait_ge(s["loaded"], 32)


def plan_steps(nc, m, a):
    with ExitStack() as ctx:
        s = sems(nc, "numbers", "keys_in", "key", "keys_out", "keys_wide", "counted", "tiles_known", "plan_out",
                 "fetched", "as_rows", "rows_out", "turned", "evacuated", "clear")
        sb = lambda name, shape, dt=F32: ctx.enter_context(nc.sbuf_tensor(name, shape, dt))
        keys = sb("keys", [P, TC, 1], I32)
        keyf = sb("keyf", [P, TC])
        tile_no = sb("tile_no", [P, TC])
        step_no = sb("step_no", [P, KC])
        tile_of = sb("tile_of", [P, KC])
        blk_of = sb("blk_of", [P, KC])
        tile_i = sb("tile_i", [P, KC], I32)
        blk_i = sb("blk_i", [P, KC], I32)
        wide = m.work[:, 0:NT - 1]
        junk = m.work[:, NT:2 * NT - 1]
        pair = m.both
        got = [pair[:, i * KC * P:(i + 1) * KC * P].rearrange("p (c e) -> p c e", c=KC) for i in range(3)]
        got_i = [got[0].bitcast(I32), got[1].bitcast(I32)]
        hh = m.h[:, :, :].rearrange("p b f -> p (b f)")
        rel = pair[:, 3 * KC * P:4 * KC * P].rearrange("p (c e) -> p c e", c=KC)
        srcf = hh[:, 0:KC * P].rearrange("p (c e) -> p c e", c=KC)
        memb = hh[:, KC * P:2 * KC * P].rearrange("p (c e) -> p c e", c=KC)
        tmp = hh[:, 2 * KC * P:3 * KC * P].rearrange("p (c e) -> p c e", c=KC)
        rows16 = m.work[:, 0:KC * P].bitcast(I16).rearrange("p (c r e) -> p c r e", c=KC, r=2)
        block = ctx.enter_context(nc.Block())

        @block.gpsimd
        def _(pool):
            g = nc.gpsimd
            g.iota(tile_no[:, :], pattern=[[P, TC]], base=0, channel_multiplier=1,
                   allow_small_or_imprecise_dtypes=True).then_inc(s["numbers"], 1)
            g.iota(step_no[:, :], pattern=[[P, KC]], base=0, channel_multiplier=1,
                   allow_small_or_imprecise_dtypes=True).then_inc(s["numbers"], 1)
            pool.wait_ge(s["tiles_known"], 1)
            for c in range(KC):
                for to, table in ((got_i[0], a["src"]), (got_i[1], a["dst"]), (got[2], a["edge_weight"])):
                    g.indirect_dma_start(to[:, c, :], None, table,
                                         bass.IndirectOffsetOnAxis(ap=tile_i[:, c:c + 1], axis=0)).then_inc(s["fetched"], 16)

        @block.sync
        def _(sp):
            sp.dma_start(keys[:, :, :], a["dst"].rearrange("(c p) e -> p c e", p=P)[:, :, P - 1:P],
                         allow_slow_non_contiguous=True).then_inc(s["keys_in"], 16)
            sp.wait_ge(s["key"], 3)
            sp.dma_start(m.tile_keys.rearrange("(c p) -> p c", p=P), keyf[:, :],
                         allow_slow_non_contiguous=True).then_inc(s["keys_out"], 16)
            sp.wait_ge(s["keys_out"], 16)
            sp.dma_start(wide, m.tile_keys[0:NT - 1].partition_broadcast(P)).then_inc(s["keys_wide"], 16)
            sp.wait_ge(s["tiles_known"], 2)
            for to, frm in ((m.step_tile, tile_i), (m.step_block, blk_i)):
                sp.dma_start(to.rearrange("(c p) -> p c", p=P), frm[:, :],
                             allow_slow_non_contiguous=True).then_inc(s["plan_out"], 16)
            sp.wait_ge(s["plan_out"], 32)
            sp.dma_start(m.block_of[:, :], m.step_block[0:K].rearrange("(a k) -> a k", a=1)).then_inc(s["plan_out"], 16)
            sp.wait_ge(s["as_rows"], 3)
            sp.dma_start(m.step_rows.rearrange("(c p) e -> p c e", p=P),
                         rows16.rearrange("p c r e -> p c (r e)")).then_inc(s["rows_out"], 16)
            sp.wait_ge(s["rows_out"], 16)
            sp.wait_ge(s["plan_out"], 48)
            sp.wait_ge(m.cleared, 16 * CLEARS * REP)

        @block.vector
        def _(dve):
            v = nc.vector
            dve.wait_ge(s["keys_in"], 16)
            v.tensor_scalar(keys[:, :, 0], keys[:, :, 0], 7, None, ALU.arith_shift_right).then_inc(s["key"], 1)
            dve.wait_ge(s["key"], 1)
            v.tensor_copy(keyf[:, :], keys[:, :, 0]).then_inc(s["key"], 1)
            dve.wait_ge(s["key"], 2)
            dve.wait_ge(s["numbers"], 2)
            v.tensor_tensor(keyf[:, :], keyf[:, :], tile_no[:, :], ALU.add).then_inc(s["key"], 1)
            dve.wait_ge(s["keys_wide"], 16)
            for c in range(KC):
                v.tensor_scalar(junk, wide, step_no[:, c:c + 1], 0.0, ALU.is_lt, ALU.add,
                                accum_out=tile_of[:, c:c + 1]).then_inc(s["counted"], 1)
                dve.wait_ge(s["counted"], c + 1)
            v.tensor_tensor(blk_of[:, :], step_no[:, :], tile_of[:, :], ALU.subtract).then_inc(s["clear"], 1)
            v.tensor_copy(tile_i[:, :], tile_of[:, :]).then_inc(s["tiles_known"], 1)
            dve.wait_ge(s["clear"], 1)
            v.tensor_scalar(blk_i[:, :], blk_of[:, :], float(NB - 1), None, ALU.min).then_inc(s["tiles_known"], 1)
            v.tensor_scalar(blk_of[:, :], blk_of[:, :], -float(P), None, ALU.mult).then_inc(s["clear"], 1)
            dve.wait_ge(s["fetched"], 16 * 3 * KC)
            dve.wait_ge(s["clear"], 2)
            v.tensor_copy(srcf, got_i[0]).then_inc(s["as_rows"], 1)
            v.tensor_copy(rel, got_i[1]).then_inc(s["clear"], 1)
            v.tensor_copy(rows16[:, :, 1, :], got_i[0]).then_inc(s["as_rows"], 1)
            dve.wait_ge(s["clear"], 3)
            v.tensor_scalar(tmp, rel, float(N), None, ALU.is_lt).then_inc(s["clear"], 1)
            dve.wait_ge(s["clear"], 4)
            for c in range(KC):
                v.tensor_scalar(rel[:, c, :], rel[:, c, :], blk_of[:, c:c + 1], None, ALU.add).then_inc(s["clear"], 1)
            dve.wait_ge(s["clear"], 4 + KC)
            v.tensor_copy(rows16[:, :, 0, :], rel).then_inc(s["as_rows"], 1)
            v.tensor_scalar(memb, rel, 0.0, None, ALU.is_ge).then_inc(s["clear"], 1)
            dve.wait_ge(s["clear"], 5 + KC)
            v.tensor_tensor(memb, memb, tmp, ALU.mult).then_inc(s["clear"], 1)
            dve.wait_ge(s["clear"], 6 + KC)
            v.tensor_scalar(tmp, rel, float(P), None, ALU.is_lt).then_inc(s["clear"], 1)
            dve.wait_ge(s["clear"], 7 + KC)
            v.tensor_tensor(memb, memb, tmp, ALU.mult).then_inc(s["clear"], 1)
            for c in range(KC):
                n = min(P, K - c * P)
                dve.wait_ge(s["turned"], c + 1)
                v.tensor_copy(m.cols[:, :, c * P:c * P + n],
                              m.psum[c % 2][:, :].rearrange("p (a k) -> p a k", a=4)[:, :, 0:n]).then_inc(s["evacuated"], 1)
            dve.wait_ge(s["evacuated"], KC)
            v.tensor_copy(m.gather_idx[:, 0:K], m.src).then_inc(s["evacuated"], 1)

        @block.tensor
        def _(pe):
            pe.wait_ge(s["as_rows"], 3)
            pe.wait_ge(s["clear"], 8 + KC)
            for c in range(KC):
                if c >= 2:
                    pe.wait_ge(s["evacuated"], c - 1)
                for i, frm in enumerate((srcf, rel, got[2], memb)):
                    last = nc.tensor.transpose(m.psum[c % 2][:, i * P:(i + 1) * P], frm[:, c, :], m.ident[:, :])
                last.then_inc(s["turned"], 1)


def layer_norm(nc, m):
    with ExitStack() as ctx:
        s = sems(nc, "ln_dve", "ln_act")
        centred = m.work[:, 0:NB * D].rearrange("p (b f) -> p b f", b=NB)
        h = m.h[:, :, 0:D]
        wide = lambda t: t[:, :].unsqueeze(2).to_broadcast([P, NB, D])
        block = ctx.enter_context(nc.Block())

        @block.vector
        def _(dve):
            v = nc.vector
            v.tensor_reduce(m.stat[:, :], m.x[:, :, :], AX, ALU.add).then_inc(s["ln_dve"], 1)
            dve.wait_ge(s["ln_dve"], 1)
            v.tensor_scalar(m.stat[:, :], m.stat[:, :], -1.0 / D, None, ALU.mult).then_inc(s["ln_dve"], 1)
            dve.wait_ge(s["ln_dve"], 2)
            v.tensor_tensor(centred, m.x[:, :, :], wide(m.stat), ALU.add).then_inc(s["ln_dve"], 1)
            dve.wait_ge(s["ln_act"], 1)
            v.tensor_reduce(m.stat2[:, :], h, AX, ALU.add).then_inc(s["ln_dve"], 1)
            dve.wait_ge(s["ln_dve"], 4)
            v.tensor_scalar(m.stat2[:, :], m.stat2[:, :], 1.0 / D, EPS, ALU.mult, ALU.add).then_inc(s["ln_dve"], 1)
            dve.wait_ge(s["ln_act"], 2)
            v.reciprocal(m.stat2[:, :], m.stat[:, :]).then_inc(s["ln_dve"], 1)
            dve.wait_ge(s["ln_dve"], 6)
            v.scalar_tensor_tensor(h, centred, 0.0, wide(m.stat2), ALU.max, ALU.mult)

        @block.scalar
        def _(act):
            act.wait_ge(s["ln_dve"], 3)
            nc.scalar.activation(h, centred, ACT.Square).then_inc(s["ln_act"], 1)
            act.wait_ge(s["ln_dve"], 5)
            nc.scalar.activation(m.stat[:, :], m.stat2[:, :], ACT.Sqrt).then_inc(s["ln_act"], 1)


BANKS = ((0, 4), (4, GP))


def group_of(array, group, lo=0, hi=GP, width=D):
    stride = array.shape[2]
    flat = array.rearrange("p b f -> p (b f)")
    part = flat[:, bass.ds(group * (GP * 2 * stride) + lo * 2 * stride, (hi - lo) * 2 * stride)]
    return part.rearrange("p (b f) -> p b f", f=stride)[:, :, 0:width]


def node_product(nc, m, sources, weight, put, row=None):
    with ExitStack() as ctx:
        s = sems(nc, "brought", "turned", "columns", "product", "put")
        together, turned = m.together, m.turned
        block = ctx.enter_context(nc.Block())

        @block.gpsimd
        def _(pool):
            pool.sem_inc(s["turned"], 2)
            with pool.Fori(0, GROUPS) as g:
                pool.wait_ge(s["turned"], after(g))
                settle(pool)
                to = together[:, :].rearrange("p (b f) -> p b f", f=D)
                if len(sources) == 1:
                    ins = nc.gpsimd.tensor_copy(to, group_of(sources[0], g))
                else:
                    ins = nc.gpsimd.tensor_tensor(to, group_of(sources[0], g), group_of(sources[1], g), ALU.add)
                ins.then_inc(s["brought"], 1)

        @block.tensor
        def _(pe):
            pe.sem_inc(s["columns"], 2)
            pe.sem_inc(s["put"], 2)
            with pe.Fori(0, GROUPS) as g:
                pe.wait_ge(s["columns"], after(g))
                pe.wait_ge(s["brought"], g + 1)
                for b, (lo, hi) in enumerate(BANKS):
                    for q in range(lo, hi):
                        last = nc.tensor.transpose(m.psum[b][:, (q - lo) * P:(q - lo + 1) * P],
                                                   together[:, q * P:(q + 1) * P], m.ident[:, :])
                    last.then_inc(s["turned"], 1)
                pe.wait_ge(s["put"], after(g))
                for b, (lo, hi) in enumerate(BANKS):
                    pe.wait_ge(s["columns"], after(g, b + 1))
                    for q in range(lo, hi):
                        to = m.psum[2 + b][:, (q - lo) * P:(q - lo + 1) * P]
                        last = nc.tensor.matmul(to, turned[:, q * P:(q + 1) * P], weight[:, :],
                                                start=True, stop=row is None)
                        if row is not None:
                            last = nc.tensor.matmul(to, m.ones[0:1, :], row[0:1, :], start=False, stop=True)
                    last.then_inc(s["product"], 1)

        @block.scalar
        def _(act):
            act.sem_inc(s["product"], 2)
            with act.Fori(0, GROUPS) as g:
                act.wait_ge(s["product"], after(g))
                for b, (lo, hi) in enumerate(BANKS):
                    act.wait_ge(s["turned"], after(g, b + 1))
                    nc.scalar.activation(turned[:, lo * P:hi * P], m.psum[b][:, 0:(hi - lo) * P],
                                         ACT.Copy).then_inc(s["columns"], 1)

        @block.vector
        def _(dve):
            with dve.Fori(0, GROUPS) as g:
                for b, (lo, hi) in enumerate(BANKS):
                    dve.wait_ge(s["product"], after(g, b + 1))
                    put(g, lo, hi, m.psum[2 + b][:, 0:(hi - lo) * P]
                        .rearrange("p (b f) -> p b f", f=D)).then_inc(s["put"], 1)


def after(g, n=0):
    return g * 2 + 2 + n


def put_rows(nc, to):
    return lambda g, lo, hi, rows: nc.vector.tensor_copy(group_of(to, g, lo, hi), rows)


def settle(engine):
    engine.nop(nofuse=True)


def run_values(nc, engine, ap, most):
    _, values = nc.values_load_multi_w_load_instructions(
        ap, engines=(engine,), min_val=0, max_val=most, skip_runtime_bounds_check_because="the plan bounds them")
    return values


def ahead(k, n):
    return k + 1 + n


def steps_by_source(nc, m, last_layer):
    with ExitStack() as ctx:
        s = sems(nc, "onehot", "same", "z", "msg", "summed", "staged", "idx", "repeat", "fix",
                 "scaled", "sum", "began", "gram_done", "junk_clear")
        rows_in = ring(nc, "rows_in", 2)
        scattered = ring(nc, "scattered", SLOTS)
        hidden_in = ring(nc, "hidden_in", 2)
        block = ctx.enter_context(nc.Block())
        H = SLOTS
        R = 4
        B = 4
        SB = 2 if last_layer else 4
        GRAM = 6

        def products(j, steps=1):
            return m.hidden_in[j // H % 2][:, j % H * D:(j % H + steps) * D]

        @block.sync
        def _(sp):
            keys = m.step_rows.rearrange("k e -> (k e)")
            sp.wait_ge(s["began"], 1)
            with sp.Fori(0, IT) as i:
                for run in range(RUNS):
                    sp.wait_ge(s["same"] if last_layer else s["repeat"], ahead(i * U + run * H + H - 1 - 2 * H, U))
                    sp.dma_start(m.rows[:, run % 2].rearrange("p s r e -> p (s r e)"),
                                 keys[bass.ds(i * (U * 2 * P) + run * (H * 2 * P), H * 2 * P)].partition_broadcast(P)
                                 ).then_inc(rows_in[run % 2], 16)
                    if last_layer:
                        sp.wait_ge(s["msg"], ahead(i * U + run * H + H - 1 - 2 * H, U))
                        sp.dma_start(m.hidden_in[run % 2], m.hidden[bass.ds((i * RUNS + run) * P, P), :]
                                     ).then_inc(hidden_in[run % 2], 16)

        @block.vector
        def _(dve):
            v = nc.vector
            v.memset(m.msg[:, :, D:RW], 1.0).then_inc(s["junk_clear"], 1)
            v.memset(m.zero[:, :], 0.0).then_inc(s["junk_clear"], 1)
            dve.wait_ge(s["began"], 1)
            v.sem_inc(s["idx"], 1)
            with dve.Fori(0, IT) as i:
                def compare(j):
                    k = i * U + j
                    run, n = divmod(j, H)
                    if n == 0:
                        dve.wait_ge(rows_in[run % 2], i * (8 * RUNS) + run // 2 * 16 + 16)
                    rel_row, src_row = m.rows[:, run % 2, n, 0, :], m.rows[:, run % 2, n, 1, :]
                    src_col = m.src[:, bass.ds(k, 1)]
                    dve.wait_ge(s["z"], ahead(k - R, R))
                    v.tensor_scalar(m.onehot[:, j % R, :], rel_row, m.part[:, :], None, ALU.is_equal).then_inc(s["onehot"], 1)
                    dve.wait_ge(s["summed"], ahead(k - R, R))
                    v.tensor_scalar(m.same[:, j % R, :], src_row, src_col, None, ALU.is_equal).then_inc(s["same"], 1)
                    if last_layer:
                        return
                    dve.wait_ge(s["repeat"], ahead(k - 2, U))
                    v.scalar_tensor_tensor(m.msg_junk[:, j % 2, :], src_row, src_col, m.before[:, :], ALU.is_equal, ALU.mult,
                                           accum_out=m.repeats[:, j:j + 1]).then_inc(s["repeat"], 1)

                def aim(run):
                    k = i * U + run * H
                    at = m.scatter_idx[:, bass.ds(k, H)]
                    if last_layer:
                        dve.wait_ge(s["staged"], ahead(k - U + 2 * H - 1, U))
                        v.tensor_copy(m.idx[run][:, :], at).then_inc(s["idx"], 1)
                        return
                    dve.wait_ge(s["repeat"], ahead(k + H - 1, U))
                    f = i * (4 * RUNS) + run * 4
                    rep, src = m.repeats[:, run * H:run * H + H], m.src[:, bass.ds(k, H)]
                    to_trash = m.small[:, 0:H]
                    dve.wait_ge(s["idx"], i * RUNS + run + 1)
                    v.tensor_scalar(rep, rep, 0.0, None, ALU.is_gt).then_inc(s["fix"], 1)
                    v.tensor_scalar(to_trash, src, -1.0, m.trash[:, :], ALU.mult, ALU.add).then_inc(s["fix"], 1)
                    dve.wait_ge(s["fix"], f + 2)
                    v.tensor_tensor(to_trash, to_trash, rep, ALU.mult).then_inc(s["fix"], 1)
                    dve.wait_ge(s["fix"], f + 3)
                    v.tensor_tensor(at, to_trash, src, ALU.add).then_inc(s["fix"], 1)
                    dve.wait_ge(s["staged"], ahead(k - U + 2 * H - 1, U))
                    v.tensor_tensor(m.idx[run][:, :], to_trash, src, ALU.add).then_inc(s["idx"], 1)

                def scale(j):
                    if j % H == 0:
                        dve.wait_ge(hidden_in[j // H % 2], i * (8 * RUNS) + j // H // 2 * 16 + 16)
                    part = products(j, R).rearrange("p (k f) -> p k f", f=D)
                    v.tensor_tensor(part, part, m.scale_row[:, 0:D].unsqueeze(1).to_broadcast([P, R, D]),
                                    ALU.mult).then_inc(s["scaled"], 1)

                def add_row(j):
                    k = i * U + j
                    dve.wait_ge(s["z"], ahead(k, R))
                    dve.wait_ge(s["scaled"], i * (U // R) + j // R + 1)
                    v.tensor_tensor(products(j), products(j), m.psum[j % B][:, 0:D], ALU.add).then_inc(s["sum"], 1)

                for j in range(U + 1):
                    if j < U:
                        compare(j)
                    if last_layer and j >= 1:
                        add_row(j - 1)
                    if j == U:
                        continue
                    if last_layer and j % R == 0:
                        scale(j)
                    if j % H == H - 1:
                        aim(j // H)

        @block.tensor
        def _(pe):
            pe.wait_ge(s["junk_clear"], 2)
            pe.sem_inc(s["z"], R)
            pe.sem_inc(s["same"], U)
            pe.sem_inc(s["repeat"], U)
            pe.sem_inc(s["staged"], U)
            pe.sem_inc(s["summed"], R)
            pe.sem_inc(s["msg"], U)
            if last_layer:
                nc.tensor.matmul(m.psum[GRAM][0:D, 0:RW], m.zero[:, 0:D], m.zero[:, 0:RW], start=True, stop=False,
                                 skip_group_check=True)
                pe.sem_inc(s["sum"], B)
            pe.sem_inc(s["began"], 1)
            with pe.Fori(0, IT) as i:
                blocks = []

                def expand(j):
                    k = i * U + j
                    pe.wait_ge(s["onehot"], k + 1)
                    if last_layer:
                        pe.wait_ge(s["sum"], ahead(k - B, B))
                    else:
                        pe.wait_ge(s["msg"], ahead(k - B, U))
                    nc.tensor.matmul(m.psum[j % B][:, 0:D], m.onehot[:, j % R, :],
                                     m.both[:, bass.ds(blocks[j] * (2 * D), D)], start=True, stop=True).then_inc(s["z"], 1)

                def sum_same(j):
                    k = i * U + j
                    pe.wait_ge(s["same"], ahead(k, U))
                    pe.wait_ge(s["msg"], ahead(k, U))
                    pe.wait_ge(s["staged"], ahead(k - SB, U))
                    if last_layer:
                        nc.tensor.matmul(m.psum[GRAM][0:D, 0:RW], m.msg[:, j % R, 0:D], m.msg[:, j % R, 0:RW],
                                         start=False, stop=False, skip_group_check=True)
                    nc.tensor.matmul(m.psum[B + j % SB][:, 0:RW], m.same[:, j % R, :], m.msg[:, j % R, 0:RW],
                                     start=True, stop=True).then_inc(s["summed"], 1)

                for j in range(U + 2):
                    if j < U and j % H == 0:
                        blocks += run_values(nc, ENG.PE, m.block_of[0:1, bass.ds(i * U + j, H)], NB - 1)
                    if j < U:
                        expand(j)
                    if j >= 2:
                        sum_same(j - 2)
            if last_layer:
                nc.tensor.matmul(m.psum[GRAM][0:D, 0:RW], m.zero[:, 0:D], m.zero[:, 0:RW], start=False, stop=True,
                                 skip_group_check=True).then_inc(s["gram_done"], 1)

        @block.scalar
        def _(act):
            a = nc.scalar
            act.wait_ge(s["began"], 1)
            def steps(i, first=False):
                def weigh(j):
                    k = i * U + j
                    act.wait_ge(s["summed"], ahead(k - R, R))
                    msg, z = m.msg[:, j % R, 0:D], m.psum[j % B][:, 0:D]
                    if last_layer:
                        act.wait_ge(s["sum"], ahead(k, B))
                        a.activation(msg, products(j), ACT.Relu).then_inc(s["msg"], 1)
                    else:
                        act.wait_ge(s["z"], ahead(k, R))
                        settle(act)
                        a.activation(m.msg[:, j % R, D:RW], m.member[:, bass.ds(k, 1)], ACT.Copy)
                        a.activation(msg, z, ACT.Copy, scale=m.wt[:, bass.ds(k, 1)]).then_inc(s["msg"], 1)

                def stage(j):
                    act.wait_ge(s["summed"], ahead(i * U + j, R))
                    if not first or j >= H:
                        act.wait_ge(scattered[j % H], i * (16 * RUNS) + (j // H) * 16)
                    a.activation(m.slot[j % H][:, 0:RW], m.psum[B + j % SB][:, 0:RW], ACT.Copy).then_inc(s["staged"], 1)

                for j in range(U + 2):
                    if j < U:
                        weigh(j)
                    if j >= 2:
                        stage(j - 2)
            steps(0, first=True)
            with act.Fori(1, IT) as i:
                steps(i)
            if last_layer:
                act.wait_ge(s["gram_done"], 1)
                a.activation(m.gram[:, :], m.psum[GRAM][0:D, 0:RW], ACT.Copy)

        @block.gpsimd
        def _(pool):
            pool.wait_ge(s["began"], 1)
            with pool.Fori(0, IT) as i:
                for j in range(U):
                    if j % H == 0:
                        pool.wait_ge(s["idx"], i * RUNS + j // H + 2)
                    pool.wait_ge(s["staged"], ahead(i * U + j, U))
                    settle(pool)
                    nc.gpsimd.indirect_dma_start(m.acc[j % REP],
                                                 bass.IndirectOffsetOnAxis(ap=m.idx[j // H][:, j % H:j % H + 1], axis=0),
                                                 m.slot[j % H][:, 0:RW], None, compute_op=ALU.add).then_inc(scattered[j % H], 16)
            for n in range(SLOTS):
                pool.wait_ge(scattered[n], IT * 16 * RUNS)


def steps_by_target(nc, m, inputs, with_attr):
    with ExitStack() as ctx:
        s = sems(nc, "onehot", "summed", "added", "idx", "message", "marked", "sum", "clear", "began", "gram_done",
                 "blank", "cleared", "projected", "held")
        gathered = ring(nc, "gathered", SLOTS)
        attr_in = ring(nc, "attr_in", SLOTS)
        hidden_out = ring(nc, "hidden_out", 2)
        block = ctx.enter_context(nc.Block())
        H, R, GRAM, HIDDEN = SLOTS, 4, 4, 4
        width = 2 * D if with_attr else RW
        clears = 2 if with_attr else 2 + SLOTS

        @block.sync
        def _(sp):
            sp.wait_ge(s["began"], 1)
            with sp.Fori(0, IT) as i:
                for run in range(RUNS):
                    tiles = run_values(nc, ENG.SP, m.step_tile[bass.ds(i * U + run * H, H)].rearrange("(a k) -> a k", a=1), NT - 1)
                    for n in range(H):
                        k = i * U + run * H + n
                        if with_attr:
                            sp.wait_ge(s["summed"], ahead(k - SLOTS, SLOTS))
                            sp.dma_start(m.slot[n][:, D:2 * D], inputs["edge_attr"][bass.ds(tiles[n] * P, P), :]
                                         ).then_inc(attr_in[n], 16)
                        else:
                            sp.wait_ge(s["projected"], ahead(k - SLOTS, SLOTS))
                            sp.dma_start(m.attr_turned[:, n * P:(n + 1) * P],
                                         inputs["attr_turned"][bass.ds(tiles[n] * D, D), :]).then_inc(attr_in[n], 16)

        @block.vector
        def _(dve):
            v = nc.vector
            v.memset(m.zero[:, :], 0.0).then_inc(s["clear"], 1)
            v.memset(m.gather_idx[:, K:K + U], 0).then_inc(s["clear"], 1)
            if not with_attr:
                for slot in m.slot:
                    v.memset(slot[:, D:RW], 1.0).then_inc(s["clear"], 1)
            dve.wait_ge(s["clear"], clears)
            for run in range(RUNS):
                v.tensor_copy(m.idx[run][:, :], m.gather_idx[:, run * H:run * H + H]).then_inc(s["idx"], 1)
            dve.wait_ge(s["began"], 1)
            v.sem_inc(s["added"], R)
            dve.wait_ge(s["blank"], 1)
            with dve.Fori(0, IT) as i:
                blocks = []

                def match(j):
                    k = i * U + j
                    dve.wait_ge(s["summed"], ahead(k - R, SLOTS))
                    v.tensor_scalar(m.onehot[:, j % R, :], m.iota_row[:, :], m.rel[:, bass.ds(k, 1)], None,
                                    ALU.is_equal).then_inc(s["onehot"], 1)

                def add_attr(j):
                    dve.wait_ge(gathered[j % H], i * (16 * RUNS) + (j // H) * 16 + 16)
                    dve.wait_ge(attr_in[j % H], i * (16 * RUNS) + (j // H) * 16 + 16)
                    slot = m.slot[j % H]
                    v.tensor_tensor(slot[:, 0:D], slot[:, 0:D], slot[:, D:2 * D], ALU.add).then_inc(s["sum"], 1)

                def add_block(j):
                    k = i * U + j
                    dve.wait_ge(s["summed"], ahead(k, SLOTS))
                    dve.wait_ge(s["added"], ahead(k - 1, R))
                    rows = m.both[:, bass.ds(blocks[j] * (2 * D), width)]
                    v.tensor_tensor(rows, rows, m.psum[j % R][:, 0:width], ALU.add).then_inc(s["added"], 1)

                for j in range(U + 2):
                    if j < U:
                        match(j)
                        if with_attr:
                            add_attr(j)
                    if j < U and j % H == 0:
                        blocks += run_values(nc, ENG.DVE, m.block_of[0:1, bass.ds(i * U + j, H)], NB - 1)
                    if j >= 2:
                        add_block(j - 2)
                    if j >= H and (j - 1) % H == 0:
                        run = j // H - 1
                        v.tensor_copy(m.idx[run][:, :], m.gather_idx[:, bass.ds(i * U + U + run * H, H)]).then_inc(s["idx"], 1)

        @block.tensor
        def _(pe):
            pe.wait_ge(s["clear"], clears)
            pe.sem_inc(s["summed"], SLOTS)
            pe.sem_inc(s["projected"], SLOTS)
            pe.sem_inc(s["held"], R)
            if with_attr:
                nc.tensor.matmul(m.psum[GRAM][0:D, 0:D], m.zero[:, 0:D], m.zero[:, 0:D], start=True, stop=False,
                                 skip_group_check=True)
            pe.sem_inc(s["began"], 1)
            with pe.Fori(0, IT) as i:
                for j in range(U):
                    k = i * U + j
                    rows = m.slot[j % H]
                    if not with_attr:
                        pe.wait_ge(s["held"], ahead(k - R, R))
                        pe.wait_ge(attr_in[j % H], i * (16 * RUNS) + (j // H) * 16 + 16)
                        nc.tensor.matmul(m.psum[HIDDEN + j % R][:, 0:D], m.attr_turned[:, j % H * P:(j % H + 1) * P],
                                         m.w1a_ea[:, :], start=True, stop=True).then_inc(s["projected"], 1)
                    pe.wait_ge(s["onehot"], k + 1)
                    pe.wait_ge(s["added"], ahead(k - R, R))
                    if with_attr:
                        pe.wait_ge(s["marked"], k + 1)
                        nc.tensor.matmul(m.psum[GRAM][0:D, 0:D], m.msg[:, j % R, 0:D], rows[:, D:2 * D],
                                         start=False, stop=False, skip_group_check=True)
                        pe.wait_ge(s["message"], k + 1)
                    else:
                        pe.wait_ge(gathered[j % H], i * (16 * RUNS) + (j // H) * 16 + 16)
                    nc.tensor.matmul(m.psum[j % R][:, 0:width], m.onehot[:, j % R, :], rows[:, 0:width],
                                     start=True, stop=True).then_inc(s["summed"], 1)
            if with_attr:
                nc.tensor.matmul(m.psum[GRAM][0:D, 0:D], m.zero[:, 0:D], m.zero[:, 0:D], start=False, stop=True,
                                 skip_group_check=True).then_inc(s["gram_done"], 1)

        @block.scalar
        def _(act):
            a = nc.scalar
            act.wait_ge(s["clear"], clears)
            a.activation(m.pair[:, :, 0:width], m.zero[:, 0:1].unsqueeze(2).to_broadcast([P, NB, width]),
                         ACT.Copy).then_inc(s["blank"], 1)
            if not with_attr:
                a.activation(m.work[:, 0:CLEAR], m.zero[:, 0:1].to_broadcast([P, CLEAR]), ACT.Copy).then_inc(s["blank"], 1)
                act.wait_ge(s["blank"], 2)
                for acc in m.acc:
                    rows = acc.rearrange("(p r) f -> p (r f)", p=P)
                    for lo in range(0, ACC_ROWS // P * RW, CLEAR):
                        act.dma_start(rows[:, lo:lo + CLEAR], m.work[:, 0:CLEAR]).then_inc(s["cleared"], 16)
            act.wait_ge(s["began"], 1)

            def message_steps(i):
                for j in range(U):
                    k = i * U + j
                    slot = m.slot[j % H]
                    act.wait_ge(s["summed"], ahead(k - R, SLOTS))
                    act.wait_ge(attr_in[j % H], i * (16 * RUNS) + (j // H) * 16 + 16)
                    settle(act)
                    a.activation(m.msg[:, j % R, 0:D], slot[:, D:2 * D], ACT.Copy,
                                 scale=m.member[:, bass.ds(k, 1)]).then_inc(s["marked"], 1)
                    act.wait_ge(s["sum"], k + 1)
                    a.activation(slot[:, 0:D], slot[:, 0:D], ACT.Relu).then_inc(s["message"], 1)

            def product_steps(i, first=False):
                for run in range(RUNS):
                    if not first or run >= 2:
                        act.wait_ge(hidden_out[run % 2], i * (8 * RUNS) + run // 2 * 16)
                    for n in range(H):
                        k = i * U + run * H + n
                        act.wait_ge(s["projected"], ahead(k, SLOTS))
                        settle(act)
                        a.activation(m.hidden_out[run % 2][:, n * D:(n + 1) * D], m.psum[HIDDEN + n % R][:, 0:D], ACT.Copy,
                                     scale=m.member[:, bass.ds(k, 1)]).then_inc(s["held"], 1)
                    act.wait_ge(s["held"], ahead(i * U + run * H + H - 1, R))
                    act.dma_start(m.hidden[bass.ds((i * RUNS + run) * P, P), :], m.hidden_out[run % 2]
                                  ).then_inc(hidden_out[run % 2], 16)

            if with_attr:
                with act.Fori(0, IT) as i:
                    message_steps(i)
                act.wait_ge(s["gram_done"], 1)
                a.activation(m.gram[:, 0:D], m.psum[GRAM][0:D, 0:D], ACT.Copy)
            else:
                product_steps(0, first=True)
                with act.Fori(1, IT) as i:
                    product_steps(i)
                for done in hidden_out:
                    act.wait_ge(done, IT * 8 * RUNS)
                act.wait_ge(s["cleared"], 16 * CLEARS * REP)

        @block.gpsimd
        def _(pool):
            pool.wait_ge(s["began"], 1)
            with pool.Fori(0, IT) as i:
                for j in range(U):
                    if j % H == 0:
                        pool.wait_ge(s["idx"], i * RUNS + j // H + 1)
                    pool.wait_ge(s["summed"], ahead(i * U + j - SLOTS, SLOTS))
                    settle(pool)
                    nc.gpsimd.indirect_dma_start(m.slot[j % H][:, 0:D], None, m.table,
                                                 bass.IndirectOffsetOnAxis(ap=m.idx[j // H][:, j % H:j % H + 1], axis=0)
                                                 ).then_inc(gathered[j % H], 16)


def load_parameters(nc, m, a):
    with ExitStack() as ctx:
        s = sems(nc, "blank", "loaded", "signed", "sums", "u_in", "u_done")
        block = ctx.enter_context(nc.Block())
        squares = {"hamilton": a["hamilton"], "l1": a["l1_w"], "l2a": a["l2_w1"], "l2b": a["l2_w2"], "l3_h": a["w1a"][0:D, :],
                   "l3_b": a["w1b"], "l3_x": a["w2a"][0:D, :], "l3_agg": a["w2a"][D:2 * D, :], "l3_out": a["w2b"]}
        columns = {"gamma": a["gamma"], "beta": a["beta"], "l2_b1": a["l2_b1"], "l2_b2": a["l2_b2"], "g2a": a["g2a"], "b2a": a["b2a"],
                   "g2b": a["g2b"], "b2b": a["b2b"]}
        rows = {"l1_bias": a["l1_bias"], "g1a": a["g1a"], "b1a": a["b1a"], "g1b": a["g1b"], "b1b": a["b1b"]}
        signs, wu = m.work[:, 0:P], m.work[0:D, P:2 * P]
        s_loads = 2 * len(squares) + 2 + 2 * len(columns) + len(rows) + 2 + 3

        @block.vector
        def _(dve):
            v = nc.vector
            for w in m.w.values():
                v.memset(w[:, :], 0.0).then_inc(s["blank"], 1)
            v.memset(signs, 0.0).then_inc(s["blank"], 1)
            v.memset(m.valid[:, :], 1.0)
            v.memset(m.twice[0:D, :], 1.0)
            v.memset(m.twice[D:P, :], 2.0)
            v.memset(m.share[0:D, :], Q * P / N)
            v.memset(m.share[D:P, :], (N - Q * P) / N)
            dve.wait_ge(s["loaded"], 16 * s_loads)
            v.tensor_tensor(m.w["hamilton"][:, :], m.w["hamilton"][:, :], signs, ALU.mult)
            dve.wait_ge(s["u_done"], 1)
            v.tensor_copy(m.col["l3_u"][:, :], m.psum[0][:, 0:1])

        @block.sync
        def _(sp):
            n = 0

            def load(to, frm):
                sp.dma_start(to, frm).then_inc(s["loaded"], 16)
                return 1

            column = lambda t: t.rearrange("(p a) -> p a", a=1)
            for name, frm in columns.items():
                n += load(m.col[name][0:D, :], column(frm)) + load(m.col[name][D:P, :], column(frm))
            for name, frm in rows.items():
                n += load(m.row[name][:, :], frm.partition_broadcast(P))
            n += load(m.w1a[:, :], a["w1a"]) + load(m.w1a_ea[:, :], a["w1a"][D:2 * D, :])
            n += load(wu[:, 0:D], a["w2a"][2 * D:3 * D, :]) + load(wu[:, D:P], a["w2a"][2 * D:3 * D, :])
            n += load(m.u0[:, :], column(a["u"][0, :]))
            sp.wait_ge(s["blank"], len(WEIGHTS) + 1)
            for name, frm in squares.items():
                n += load(m.w[name][0:D, 0:D], frm) + load(m.w[name][D:P, D:P], frm)
            n += load(signs[0:D, 0:D], a["signs"]) + load(signs[D:P, D:P], a["signs"])
            assert n == s_loads, (n, s_loads)

        @block.tensor
        def _(pe):
            pe.wait_ge(s["loaded"], 16 * s_loads)
            nc.tensor.matmul(m.psum[0][:, 0:1], wu, m.u0[:, :], start=True, stop=True).then_inc(s["u_done"], 1)


def sum_copies(nc, m):
    with ExitStack() as ctx:
        s = sems(nc, "added", "added_pool")
        came = ring(nc, "came", REP)
        size = NB * RW
        places = [m.both[:, 0:size], m.both[:, size:2 * size], m.work[:, 0:size]]
        cut = NB * 2 // 3 * RW
        block = ctx.enter_context(nc.Block())
        where = lambda r: places[0] if r == 0 else places[1 + (r - 1) % 2]

        @block.sync
        def _(sp):
            for r in range(REP):
                if r >= 3:
                    sp.wait_ge(s["added"], r - 2)
                    sp.wait_ge(s["added_pool"], r - 2)
                sp.dma_start(where(r).rearrange("p (b f) -> p b f", f=RW), node_rows(m.acc[r], 0, NB)).then_inc(came[r], 16)

        def add(engine, ops, done, lo, hi):
            engine.wait_ge(came[0], 16)
            for r in range(1, REP):
                engine.wait_ge(came[r], 16)
                if r > 1:
                    engine.wait_ge(done, r - 1)
                to = places[0][:, lo:hi]
                ops.tensor_tensor(to, to, where(r)[:, lo:hi], ALU.add).then_inc(done, 1)

        @block.vector
        def _(dve):
            add(dve, nc.vector, s["added"], 0, cut)

        @block.gpsimd
        def _(pool):
            add(pool, nc.gpsimd, s["added_pool"], cut, size)


def columns_of(nc, m, terms, to, func=ACT.Copy, bias=None):
    T = len(terms)
    with ExitStack() as ctx:
        s = sems(nc, "brought", "turned", "columns", "product", "put")
        together, turned = m.together, m.turned
        block = ctx.enter_context(nc.Block())

        @block.gpsimd
        def _(pool):
            pool.sem_inc(s["turned"], 2)
            with pool.Fori(0, GROUPS) as g:
                for n, (sources, _w) in enumerate(terms):
                    pool.wait_ge(s["turned"], after(g * T + n))
                    settle(pool)
                    rows = together[:, :].rearrange("p (b f) -> p b f", f=D)
                    if len(sources) == 1:
                        ins = nc.gpsimd.tensor_copy(rows, group_of(sources[0], g))
                    else:
                        ins = nc.gpsimd.tensor_tensor(rows, group_of(sources[0], g), group_of(sources[1], g), ALU.add)
                    ins.then_inc(s["brought"], 1)

        @block.tensor
        def _(pe):
            pe.sem_inc(s["columns"], 2)
            pe.sem_inc(s["put"], 2)
            with pe.Fori(0, GROUPS) as g:
                for n, (_s, weight) in enumerate(terms):
                    pe.wait_ge(s["columns"], after(g * T + n))
                    pe.wait_ge(s["brought"], g * T + n + 1)
                    for b, (lo, hi) in enumerate(BANKS):
                        for q in range(lo, hi):
                            last = nc.tensor.transpose(m.psum[b][:, (q - lo) * P:(q - lo + 1) * P],
                                                       together[:, q * P:(q + 1) * P], m.ident[:, :])
                        last.then_inc(s["turned"], 1)
                    if weight is None:
                        continue
                    if n == 0:
                        pe.wait_ge(s["put"], after(g))
                    for b, (lo, hi) in enumerate(BANKS):
                        pe.wait_ge(s["columns"], after(g * T + n, b + 1))
                        nc.tensor.matmul(m.psum[2 + b][:, 0:(hi - lo) * P], weight[:, :], turned[:, lo * P:hi * P],
                                         start=n == 0, stop=n == T - 1).then_inc(s["product"], 1)

        @block.scalar
        def _(act):
            a = nc.scalar
            kw = {} if bias is None else {"bias": bias[:, :]}
            act.sem_inc(s["product"], 2)
            with act.Fori(0, GROUPS) as g:
                part = lambda lo, hi: to[:, bass.ds(g * (GP * P) + lo * P, (hi - lo) * P)]
                for n, (_s, weight) in enumerate(terms):
                    if weight is not None:
                        act.wait_ge(s["product"], after(g * T + n))
                    for b, (lo, hi) in enumerate(BANKS):
                        act.wait_ge(s["turned"], after(g * T + n, b + 1))
                        if weight is None:
                            settle(act)
                        a.activation(part(lo, hi) if weight is None else turned[:, lo * P:hi * P],
                                     m.psum[b][:, 0:(hi - lo) * P], ACT.Copy).then_inc(s["columns"], 1)
                if terms[0][1] is not None:
                    for b, (lo, hi) in enumerate(BANKS):
                        act.wait_ge(s["product"], after(g * T + T - 1, b + 1))
                        settle(act)
                        a.activation(part(lo, hi), m.psum[2 + b][:, 0:(hi - lo) * P], func, **kw).then_inc(s["put"], 1)


def product_of_columns(nc, m, frm, weight, to, bias=None):
    with ExitStack() as ctx:
        s = sems(nc, "product", "put")
        block = ctx.enter_context(nc.Block())

        @block.tensor
        def _(pe):
            pe.sem_inc(s["put"], 2)
            with pe.Fori(0, GROUPS) as g:
                for b, (lo, hi) in enumerate(BANKS):
                    pe.wait_ge(s["put"], after(g))
                    nc.tensor.matmul(m.psum[b][:, 0:(hi - lo) * P], weight[:, :],
                                     frm[:, bass.ds(g * (GP * P) + lo * P, (hi - lo) * P)],
                                     start=True, stop=True).then_inc(s["product"], 1)

        @block.scalar
        def _(act):
            with act.Fori(0, GROUPS) as g:
                for b, (lo, hi) in enumerate(BANKS):
                    act.wait_ge(s["product"], g * 2 + b + 1)
                    settle(act)
                    kw = {} if bias is None else {"bias": bias[:, :]}
                    nc.scalar.activation(to[:, bass.ds(g * (GP * P) + lo * P, (hi - lo) * P)],
                                         m.psum[b][:, 0:(hi - lo) * P],
                                         ACT.Copy if bias is None else ACT.Identity, **kw).then_inc(s["put"], 1)


def add_columns(nc, m, frm):
    with ExitStack() as ctx:
        s = sems(nc, "brought", "turned", "put")
        block = ctx.enter_context(nc.Block())

        @block.gpsimd
        def _(pool):
            pool.sem_inc(s["turned"], 2)
            with pool.Fori(0, GROUPS) as g:
                pool.wait_ge(s["turned"], after(g))
                settle(pool)
                nc.gpsimd.tensor_copy(m.together, frm[:, bass.ds(g * (GP * P), GP * P)]).then_inc(s["brought"], 1)

        @block.tensor
        def _(pe):
            pe.sem_inc(s["put"], 2)
            with pe.Fori(0, GROUPS) as g:
                pe.wait_ge(s["brought"], g + 1)
                pe.wait_ge(s["put"], after(g))
                for b, (lo, hi) in enumerate(BANKS):
                    for q in range(lo, hi):
                        last = nc.tensor.transpose(m.psum[b][:, (q - lo) * P:(q - lo + 1) * P],
                                                   m.together[:, q * P:(q + 1) * P], m.ident[:, :])
                    last.then_inc(s["turned"], 1)

        @block.vector
        def _(dve):
            with dve.Fori(0, GROUPS) as g:
                for b, (lo, hi) in enumerate(BANKS):
                    dve.wait_ge(s["turned"], after(g, b + 1))
                    x = group_of(m.x, g, lo, hi)
                    nc.vector.tensor_tensor(x, x, m.psum[b][:, 0:(hi - lo) * P].rearrange("p (b f) -> p b f", f=D),
                                            ALU.add).then_inc(s["put"], 1)


def batch_norm(nc, m, t, gamma, beta, func):
    with ExitStack() as ctx:
        s = sems(nc, "stats", "step", "folded", "rooted")
        whole, rest = divmod(Q * P, 512)
        chunks = whole + 1
        stats, mv = m.small[:, 0:chunks * 6], m.small[:, 6 * chunks:6 * chunks + 2]
        c = [m.small[:, 6 * chunks + 2 + i:6 * chunks + 3 + i] for i in range(5)]
        block = ctx.enter_context(nc.Block())

        @block.vector
        def _(dve):
            v = nc.vector
            for n in range(whole):
                v.bn_stats(stats[:, 6 * n:6 * n + 6], t[:, n * 512:(n + 1) * 512]).then_inc(s["stats"], 1)
            v.bn_stats(stats[0:D, 6 * whole:6 * chunks], t[0:D, whole * 512:Q * P]).then_inc(s["stats"], 1)
            v.bn_stats(stats[D:P, 6 * whole:6 * chunks], t[D:P, whole * 512:(Q - 1) * P + LAST]).then_inc(s["stats"], 1)
            dve.wait_ge(s["stats"], whole + 2)
            v.bn_aggr(mv, stats).then_inc(s["step"], 1)
            dve.wait_ge(s["step"], 1)
            v.tensor_tensor(c[0], mv[:, 0:1], m.share[:, :], ALU.mult).then_inc(s["step"], 1)
            dve.wait_ge(s["folded"], 1)
            v.tensor_copy(c[1], m.psum[0][:, 0:1]).then_inc(s["step"], 1)
            dve.wait_ge(s["step"], 3)
            v.tensor_tensor(c[2], mv[:, 0:1], c[1], ALU.subtract).then_inc(s["step"], 1)
            dve.wait_ge(s["step"], 4)
            v.tensor_tensor(c[2], c[2], c[2], ALU.mult).then_inc(s["step"], 1)
            dve.wait_ge(s["step"], 5)
            v.tensor_tensor(c[2], c[2], mv[:, 1:2], ALU.add).then_inc(s["step"], 1)
            dve.wait_ge(s["step"], 6)
            v.tensor_tensor(c[0], c[2], m.share[:, :], ALU.mult).then_inc(s["step"], 1)
            dve.wait_ge(s["folded"], 2)
            v.tensor_scalar(c[3], m.psum[1][:, 0:1], EPS, None, ALU.add).then_inc(s["step"], 1)
            dve.wait_ge(s["rooted"], 1)
            v.reciprocal(c[3], c[4]).then_inc(s["step"], 1)
            dve.wait_ge(s["step"], 9)
            v.tensor_tensor(m.col["scale"][:, :], c[3], gamma[:, :], ALU.mult).then_inc(s["step"], 1)
            dve.wait_ge(s["step"], 10)
            v.tensor_tensor(c[2], c[1], m.col["scale"][:, :], ALU.mult).then_inc(s["step"], 1)
            dve.wait_ge(s["step"], 11)
            v.tensor_tensor(m.col["shift"][:, :], beta[:, :], c[2], ALU.subtract).then_inc(s["step"], 1)

        @block.tensor
        def _(pe):
            for n, at in enumerate((2, 7)):
                pe.wait_ge(s["step"], at)
                nc.tensor.matmul(m.psum[n][:, 0:1], m.fold[:, :], c[0], start=True, stop=True).then_inc(s["folded"], 1)

        @block.scalar
        def _(act):
            act.wait_ge(s["step"], 8)
            nc.scalar.activation(c[4], c[3], ACT.Sqrt).then_inc(s["rooted"], 1)
            act.wait_ge(s["step"], 12)
            nc.scalar.activation(t[:, 0:Q * P], t[:, 0:Q * P], func, bias=m.col["shift"][:, :],
                                 scale=m.col["scale"][:, :])


def scale_by_degree_out(nc, m):
    with ExitStack() as ctx:
        s = sems(nc, "step", "rooted")
        block = ctx.enter_context(nc.Block())

        @block.vector
        def _(dve):
            v = nc.vector
            v.tensor_scalar(m.stat[:, :], m.dout[:, :], 1.0, None, ALU.max).then_inc(s["step"], 1)
            dve.wait_ge(s["rooted"], 1)
            v.reciprocal(m.stat[:, :], m.stat2[:, :]).then_inc(s["step"], 1)
            dve.wait_ge(s["step"], 2)
            h = m.h[:, :, 0:D]
            v.tensor_tensor(h, h, m.stat[:, :].unsqueeze(2).to_broadcast([P, NB, D]), ALU.mult)

        @block.scalar
        def _(act):
            act.wait_ge(s["step"], 1)
            nc.scalar.activation(m.stat2[:, :], m.stat[:, :], ACT.Sqrt).then_inc(s["rooted"], 1)


def keep_table(nc, m, rows):
    with ExitStack() as ctx:
        s = sems(nc, "kept")
        block = ctx.enter_context(nc.Block())

        @block.sync
        def _(sp):
            sp.dma_start(node_rows(m.table, 0, NB), rows).then_inc(s["kept"], 16)
            sp.wait_ge(s["kept"], 16)


def finish_second_layer(nc, m):
    with ExitStack() as ctx:
        s = sems(nc, "step", "rooted")
        block = ctx.enter_context(nc.Block())
        work = m.work[:, 0:NB * D].rearrange("p (b f) -> p b f", b=NB)

        @block.vector
        def _(dve):
            v = nc.vector
            v.tensor_copy(m.din[:, :].unsqueeze(2), m.pair[:, :, D:RW]).then_inc(s["step"], 1)
            dve.wait_ge(s["step"], 1)
            v.tensor_scalar(m.stat[:, :], m.din[:, :], 1.0, None, ALU.max).then_inc(s["step"], 1)
            dve.wait_ge(s["rooted"], 1)
            v.reciprocal(m.stat[:, :], m.stat2[:, :]).then_inc(s["step"], 1)
            dve.wait_ge(s["step"], 3)
            v.tensor_tensor(work, m.pair[:, :, 0:D], m.stat[:, :].unsqueeze(2).to_broadcast([P, NB, D]),
                            ALU.mult).then_inc(s["step"], 1)
            v.tensor_tensor(m.x[:, :, :], m.x[:, :, :], m.row["l1_bias"][:, :].unsqueeze(1).to_broadcast([P, NB, D]),
                            ALU.add).then_inc(s["step"], 1)
            dve.wait_ge(s["step"], 5)
            v.tensor_tensor(m.x[:, :, :], m.x[:, :, :], work, ALU.add)

        @block.scalar
        def _(act):
            act.wait_ge(s["step"], 2)
            nc.scalar.activation(m.stat2[:, :], m.stat[:, :], ACT.Sqrt).then_inc(s["rooted"], 1)


def norm_rows(nc, dve, m, s, first, mean, square, count):
    v = nc.vector
    mu, var, tmp = (m.small[:, i * D:(i + 1) * D] for i in range(3))
    n = first

    def link(ins):
        nonlocal n
        ins.then_inc(s["step"], 1)
        n += 1
        dve.wait_ge(s["step"], n)

    link(v.tensor_scalar(mu, mean, 1.0 / count, None, ALU.mult))
    link(v.tensor_tensor(tmp, mu, mu, ALU.mult))
    link(v.tensor_scalar(var, square, 1.0 / count, None, ALU.mult))
    link(v.tensor_tensor(var, var, tmp, ALU.subtract))
    link(v.tensor_scalar(var, var, 0.0, EPS, ALU.max, ALU.add))
    return n, mu, var, tmp, link


def rows_of_norm(nc, dve, s, m, gamma, beta, mu, var, tmp, link):
    v = nc.vector
    link(v.reciprocal(tmp, m.small[:, 3 * D:4 * D]))
    link(v.tensor_tensor(m.scale_row[:, 0:D], tmp, gamma[:, :], ALU.mult))
    link(v.tensor_copy(m.scale_row[:, D:P], m.scale_row[:, 0:D]))
    link(v.tensor_tensor(tmp, mu, m.scale_row[:, 0:D], ALU.mult))
    link(v.tensor_tensor(m.shift_row[:, 0:D], beta[:, :], tmp, ALU.subtract))
    link(v.tensor_copy(m.shift_row[:, D:P], m.shift_row[:, 0:D]))


def norm_of_edge_input(nc, m):
    with ExitStack() as ctx:
        s = sems(nc, "step", "ready", "brought", "group", "sums", "kept", "turned", "scaled", "formed",
                 "squares", "products", "rooted")
        block = ctx.enter_context(nc.Block())
        left = m.pair[:, :, 0:D]
        group = m.compared[:, 0:2 * GP * RW]
        sums = m.work[0:RW, 0:P]
        wide_sum = m.work[:, P:2 * P]
        prod, prod_ea = m.work[0:D, 2 * P:2 * P + D], m.work[0:D, 2 * P + D:3 * P]

        @block.vector
        def _(dve):
            v = nc.vector
            v.memset(m.h[:, :, D:RW], 1.0).then_inc(s["ready"], 1)
            dve.wait_ge(s["ready"], 2)
            v.tensor_scalar(m.h[:, NB - 1, :], m.h[:, NB - 1, :], m.valid[:, :], None, ALU.mult).then_inc(s["ready"], 1)
            dve.wait_ge(s["ready"], 3)
            v.tensor_tensor(left, m.h[:, :, 0:D], m.din[:, :].unsqueeze(2).to_broadcast([P, NB, D]),
                            ALU.mult).then_inc(s["ready"], 1)
            dve.wait_ge(s["sums"], 1)
            v.tensor_copy(sums, m.psum[0][0:RW, 0:P]).then_inc(s["kept"], 1)
            dve.wait_ge(s["turned"], 1)
            v.tensor_scalar(m.turned_gram[:, 0:D], m.psum[1][:, 0:D], m.twice[:, :], None, ALU.mult).then_inc(s["scaled"], 1)
            v.tensor_copy(m.turned_gram[:, D:RW], m.psum[1][:, D:RW]).then_inc(s["scaled"], 1)
            dve.wait_ge(s["scaled"], 2)
            v.tensor_scalar(wide_sum, m.ones[:, :], m.turned_gram[:, D:RW], None, ALU.mult).then_inc(s["scaled"], 1)
            dve.wait_ge(s["formed"], 1)
            v.tensor_tensor(prod, m.psum[2][0:D, 0:D], m.w1a[0:D, :], ALU.mult).then_inc(s["squares"], 1)
            dve.wait_ge(s["formed"], 2)
            v.tensor_tensor(prod_ea, m.psum[3][0:D, 0:D], m.w1a_ea[:, :], ALU.mult).then_inc(s["squares"], 1)
            dve.wait_ge(s["products"], 2)
            n, mu, var, tmp, link = norm_rows(nc, dve, m, s, 0, m.psum[4][:, 0:D], m.psum[5][:, 0:D], E)
            dve.wait_ge(s["rooted"], 1)
            rows_of_norm(nc, dve, s, m, m.row["g1a"], m.row["b1a"], mu, var, tmp, link)
            v.tensor_tensor(m.w["l3_h"][:, :], m.w["l3_h"][:, :], m.scale_row[:, :], ALU.mult)

        @block.gpsimd
        def _(pool):
            nc.gpsimd.affine_select(out=m.valid[:, :], in_=m.valid[:, :], compare_op=ALU.is_gt, fill=0.0,
                                    base=LAST, pattern=[[0, 1]], channel_multiplier=-1).then_inc(s["ready"], 1)
            pool.wait_ge(s["ready"], 4)
            pool.sem_inc(s["group"], 1)
            with pool.Fori(0, GROUPS) as g:
                pool.wait_ge(s["group"], g + 1)
                settle(pool)
                nc.gpsimd.tensor_copy(group.rearrange("p (b f) -> p b f", f=RW), group_of(m.h, g, width=RW)).then_inc(s["brought"], 1)

        @block.tensor
        def _(pe):
            nc.tensor.matmul(m.psum[0][0:RW, 0:P], m.zero[:, 0:RW], m.ones[:, :], start=True, stop=False,
                             skip_group_check=True)
            pe.wait_ge(s["ready"], 4)
            with pe.Fori(0, GROUPS) as g:
                pe.wait_ge(s["brought"], g + 1)
                for b in range(2 * GP):
                    last = nc.tensor.matmul(m.psum[0][0:RW, 0:P], group[:, b * RW:(b + 1) * RW],
                                            m.both[:, bass.ds(g * (2 * GP * 2 * D) + b * 2 * D, 2 * D)],
                                            start=False, stop=False, skip_group_check=True)
                last.then_inc(s["group"], 1)
            nc.tensor.matmul(m.psum[0][0:RW, 0:P], m.zero[:, 0:RW], m.ones[:, :], start=False, stop=True,
                             skip_group_check=True).then_inc(s["sums"], 1)
            pe.wait_ge(s["kept"], 1)
            nc.tensor.transpose(m.psum[1][:, 0:RW], sums, m.ident[0:RW, 0:RW]).then_inc(s["turned"], 1)
            pe.wait_ge(s["scaled"], 3)
            nc.tensor.matmul(m.psum[2][0:D, 0:D], m.turned_gram[:, 0:D], m.w1a[:, :], start=True, stop=True).then_inc(s["formed"], 1)
            nc.tensor.matmul(m.psum[3][0:D, 0:D], m.gram[:, 0:D], m.w1a_ea[:, :], start=True, stop=True).then_inc(s["formed"], 1)
            nc.tensor.matmul(m.psum[4][:, 0:D], wide_sum, m.w1a[:, :], start=True, stop=True).then_inc(s["products"], 1)
            pe.wait_ge(s["squares"], 2)
            nc.tensor.matmul(m.psum[5][:, 0:D], m.ones[0:D, :], prod, start=True, stop=False)
            nc.tensor.matmul(m.psum[5][:, 0:D], m.ones[0:D, :], prod_ea, start=False, stop=True).then_inc(s["products"], 1)

        @block.scalar
        def _(act):
            act.wait_ge(s["step"], 5)
            nc.scalar.activation(m.small[:, 3 * D:4 * D], m.small[:, D:2 * D], ACT.Sqrt).then_inc(s["rooted"], 1)


def norm_of_edge_output(nc, m):
    with ExitStack() as ctx:
        s = sems(nc, "step", "widened", "formed", "squares", "products", "rooted", "mean")
        block = ctx.enter_context(nc.Block())
        w = m.w["l3_b"]
        wide_sum, prod = m.work[0:D, 0:P], m.work[0:D, P:P + D]

        @block.vector
        def _(dve):
            v = nc.vector
            v.tensor_scalar(wide_sum, m.ones[0:D, :], m.gram[:, D:RW], None, ALU.mult).then_inc(s["widened"], 1)
            dve.wait_ge(s["formed"], 1)
            v.tensor_tensor(prod, m.psum[0][0:D, 0:D], w[0:D, 0:D], ALU.mult).then_inc(s["squares"], 1)
            dve.wait_ge(s["products"], 2)
            n, mu, var, tmp, link = norm_rows(nc, dve, m, s, 0, m.psum[1][:, 0:D], m.psum[2][:, 0:D], E)
            dve.wait_ge(s["rooted"], 1)
            rows_of_norm(nc, dve, s, m, m.row["g1b"], m.row["b1b"], mu, var, tmp, link)
            v.tensor_tensor(w[:, :], w[:, :], m.scale_row[:, :], ALU.mult)
            v.tensor_scalar(m.stat[:, :], m.dout[:, :], 1.0, None, ALU.max).then_inc(s["mean"], 1)
            dve.wait_ge(s["mean"], 1)
            v.reciprocal(m.stat2[:, :], m.stat[:, :]).then_inc(s["mean"], 1)
            dve.wait_ge(s["mean"], 2)
            sums = m.both[:, 0:NB * RW].rearrange("p (b f) -> p b f", f=RW)[:, :, 0:D]
            v.tensor_tensor(sums, sums, m.stat2[:, :].unsqueeze(2).to_broadcast([P, NB, D]), ALU.mult)
            v.tensor_scalar(m.din[:, :], m.dout[:, :], 1.0, None, ALU.min)

        @block.tensor
        def _(pe):
            nc.tensor.matmul(m.psum[0][0:D, 0:D], m.gram[:, 0:D], w[0:D, 0:D], start=True, stop=True).then_inc(s["formed"], 1)
            pe.wait_ge(s["widened"], 1)
            nc.tensor.matmul(m.psum[1][:, 0:D], wide_sum, w[0:D, 0:D], start=True, stop=True).then_inc(s["products"], 1)
            pe.wait_ge(s["squares"], 1)
            nc.tensor.matmul(m.psum[2][:, 0:D], m.ones[0:D, :], prod, start=True, stop=True).then_inc(s["products"], 1)

        @block.scalar
        def _(act):
            act.wait_ge(s["step"], 5)
            nc.scalar.activation(m.small[:, 3 * D:4 * D], m.small[:, D:2 * D], ACT.Sqrt).then_inc(s["rooted"], 1)


def keep_degree_out(nc, m):
    with ExitStack() as ctx:
        block = ctx.enter_context(nc.Block())

        @block.vector
        def _(dve):
            sums = m.both[:, 0:NB * RW].rearrange("p (b f) -> p b f", f=RW)
            nc.vector.tensor_copy(m.dout[:, :].unsqueeze(2), sums[:, :, D:RW])


def store(nc, m, out):
    with ExitStack() as ctx:
        s = sems(nc, "stored")
        block = ctx.enter_context(nc.Block())

        @block.sync
        def _(sp):
            sp.dma_start(node_rows(out, 0, NB - 1), m.x[:, 0:NB - 1, :]).then_inc(s["stored"], 16)
            sp.dma_start(out[(NB - 1) * P:N, :], m.x[0:LAST, NB - 1, :]).then_inc(s["stored"], 16)
            sp.wait_ge(s["stored"], 32)


def gnn_stack(nc, a, out):
    with ExitStack() as ctx:
        m = allocate(nc, ctx)
        first = m.both[:, 0:NB * RW].rearrange("p (b f) -> p b f", f=RW)
        second = m.both[:, NB * RW:NB * RW + NB * D].rearrange("p (b f) -> p b f", f=D)
        work = m.work[:, 0:NB * D]
        columns_in_h = m.h[:, :, :].rearrange("p b f -> p (b f)")[:, 0:NB * D]

        with nc.cleanup_on_exit():
            m.cleared = nc.alloc_semaphore(name="cleared")
            constants_and_nodes(nc, m, a)
            load_parameters(nc, m, a)
            plan_steps(nc, m, a)

            layer_norm(nc, m)
            node_product(nc, m, [m.h], m.w["hamilton"], put_rows(nc, m.pair))
            steps_by_source(nc, m, last_layer=False)
            sum_copies(nc, m)
            keep_degree_out(nc, m)
            columns_of(nc, m, [([first], None)], work)
            batch_norm(nc, m, work, m.col["gamma"], m.col["beta"], ACT.Tanh)
            add_columns(nc, m, work)

        with nc.cleanup_on_exit():
            layer_norm(nc, m)
            scale_by_degree_out(nc, m)
            node_product(nc, m, [m.h], m.w["l1"], put_rows(nc, work.rearrange("p (b f) -> p b f", f=D)))
            keep_table(nc, m, work.rearrange("p (b f) -> p b f", f=D))
            steps_by_target(nc, m, a, with_attr=False)
            finish_second_layer(nc, m)

        with nc.cleanup_on_exit():
            layer_norm(nc, m)
            keep_table(nc, m, m.h[:, :, 0:D])
            steps_by_target(nc, m, a, with_attr=True)
            columns_of(nc, m, [([m.h, m.pair], m.w["l2a"])], work, ACT.Relu, m.col["l2_b1"])
            product_of_columns(nc, m, work, m.w["l2b"], columns_in_h, m.col["l2_b2"])
            add_columns(nc, m, columns_in_h)

        with nc.cleanup_on_exit():
            layer_norm(nc, m)
            norm_of_edge_input(nc, m)
            node_product(nc, m, [m.h], m.w["l3_h"], put_rows(nc, m.pair), row=m.shift_row)
            steps_by_source(nc, m, last_layer=True)
            sum_copies(nc, m)
            norm_of_edge_output(nc, m)
            has_edge = lambda g, lo, hi: m.din[:, bass.ds(g * (2 * GP) + 2 * lo, 2 * (hi - lo))].unsqueeze(2)\
                .to_broadcast([P, 2 * (hi - lo), D])
            node_product(nc, m, [first], m.w["l3_b"],
                         lambda g, lo, hi, rows: nc.vector.tensor_tensor(group_of(second, g, lo, hi), rows, has_edge(g, lo, hi),
                                                                         ALU.mult), row=m.shift_row)
            columns_of(nc, m, [([m.h], m.w["l3_x"]), ([second], m.w["l3_agg"])], work, ACT.Identity, m.col["l3_u"])
            batch_norm(nc, m, work, m.col["g2a"], m.col["b2a"], ACT.Relu)
            product_of_columns(nc, m, work, m.w["l3_out"], columns_in_h)
            batch_norm(nc, m, columns_in_h, m.col["g2b"], m.col["b2b"], ACT.Identity)
            add_columns(nc, m, columns_in_h)
            store(nc, m, out)


_SHAPE = (N, D)


def kernel(**inputs):
    import numpy as np
    import concourse.bacc as bacc
    from concourse.bass_utils import run_bass_kernel_spmd

    nc = bacc.Bacc("TRN2", target_bir_lowering=False, num_devices=1)
    arrays = {}
    given = {}

    def give(name, array):
        array = np.ascontiguousarray(array)
        arrays[f"in_{name}"] = array
        given[name] = nc.dram_tensor(f"in_{name}", array.shape, mybir.dt.from_np(array.dtype), kind="ExternalInput").ap()

    for name, fill in (("src", PAD_SOURCE), ("dst", PAD_TARGET), ("edge_weight", 0)):
        give(name, np.pad(np.asarray(inputs[name]), (0, EP - E), constant_values=fill).reshape(TC * P, P))
    attr = np.pad(np.asarray(inputs["edge_attr_64"]), ((0, NT * P - E), (0, 0)))
    give("edge_attr", attr)
    give("attr_turned", attr.reshape(NT, P, D).transpose(0, 2, 1).reshape(NT * D, P))
    names = {"x": "x",
             "gamma": "L0_gnn_gamma", "beta": "L0_gnn_beta", "l1_w": "L1_gnn_weight", "l1_bias": "L1_gnn_bias",
             "l2_w1": "L2_gnn_W1", "l2_b1": "L2_gnn_b1", "l2_w2": "L2_gnn_W2", "l2_b2": "L2_gnn_b2", "u": "L3_gnn_u",
             "w1a": "L3_gnn_W1a", "g1a": "L3_gnn_g1a", "b1a": "L3_gnn_b1a", "w1b": "L3_gnn_W1b", "g1b": "L3_gnn_g1b",
             "b1b": "L3_gnn_b1b", "w2a": "L3_gnn_W2a", "g2a": "L3_gnn_g2a", "b2a": "L3_gnn_b2a", "w2b": "L3_gnn_W2b",
             "g2b": "L3_gnn_g2b", "b2b": "L3_gnn_b2b"}
    for name, theirs in names.items():
        give(name, inputs[theirs])
    part = np.array([[0, 1, 2, 3], [1, 0, 3, 2], [2, 3, 0, 1], [3, 2, 1, 0]])
    sign = np.array([[1, -1, -1, -1], [1, 1, -1, 1], [1, 1, 1, -1], [1, -1, 1, 1]], np.float32)
    n = np.arange(D)
    place = np.empty(D, np.int64)
    place[n * 4 % D + n * 4 // D] = n
    row, col = np.meshgrid(place, place, indexing="ij")
    quarter = D // 4
    weight = np.asarray(inputs["L0_gnn_weight"])
    give("hamilton", weight[row % quarter, part[row // quarter, col // quarter] * quarter + col % quarter])
    give("signs", sign[row // quarter, col // quarter])
    out = nc.dram_tensor("out_0", _SHAPE, F32, kind="ExternalOutput").ap()
    gnn_stack(nc, given, out)
    r = run_bass_kernel_spmd(nc, [arrays], core_ids=[0])
    return r.results[0]["out_0"]
```

```python
from contextlib import ExitStack

import concourse.bass as bass
from concourse import mybir

F32 = mybir.dt.float32
I32 = mybir.dt.int32
I16 = mybir.dt.int16
ALU = mybir.AluOpType
ACT = mybir.ActivationFunctionType
AX = mybir.AxisListType.X
ENG = mybir.EngineType

P = 128
N = 12500
E = 212500
D = 64
NB = -(-N // P)
NP = NB * P
LAST = N - (NB - 1) * P
NT = -(-E // P)
TC = -(-NT // P)
EP = TC * P * P
PAD_SOURCE = NP - 1
U = 32
K = -(-(NT + NB - 1) // U) * U
IT = K // U
KC = -(-K // P)
PAD_TARGET = (K - NT + 1) * P
RW = D + 1
REP = 8
ACC_ROWS = NP + P
Q = NB // 2
GP = 7
GROUPS = Q // GP
EPS = 1e-5
CLEAR_ROWS = 3
assert ACC_ROWS // P % CLEAR_ROWS == 0
PIECE = ACC_ROWS * RW // (IT * P)
assert PIECE * IT * P == ACC_ROWS * RW
SLOTS = 8
RUNS = U // SLOTS

WEIGHTS = ("hamilton", "l1", "l2a", "l2b", "l3_h", "l3_b", "l3_x", "l3_agg", "l3_out")
VECTORS = ("gamma", "beta", "l2_b1", "l2_b2", "l3_u", "g2a", "b2a", "g2b", "b2b", "scale", "shift")
ROWS = ("l1_bias", "g1a", "b1a", "g1b", "b1b")


class Memory:
    pass


SERIAL = []


def new_semaphore(nc, name):
    SERIAL.append(name)
    return nc.alloc_semaphore(name=f"{name}_{len(SERIAL)}")


def sems(nc, *names):
    return {n: new_semaphore(nc, n) for n in names}


def ring(nc, name, n):
    return [new_semaphore(nc, f"{name}{i}_") for i in range(n)]


def node_rows(ap, lo, hi):
    return ap[lo * P:hi * P, :].rearrange("(b p) f -> p b f", p=P)


def allocate(nc, ctx):
    def sb(name, shape, dt=F32):
        return ctx.enter_context(nc.sbuf_tensor(name, shape, dt))

    def dram(name, shape, dt=F32):
        return nc.dram_tensor(name, shape, dt).ap()

    m = Memory()
    m.x = sb("x_nodes", [P, NB, D])
    m.h = sb("h_nodes", [P, NB, RW])
    m.both = sb("pair_nodes", [P, 2 * NB * RW])
    m.pair = m.both[:, 0:NB * 2 * D].rearrange("p (b f) -> p b f", b=NB)
    m.work = sb("work_nodes", [P, NB * RW])
    m.cols = sb("step_cols", [P, 4, K])
    m.src, m.rel, m.wt, m.member = (m.cols[:, i, :] for i in range(4))
    m.gather_idx = sb("gather_idx", [P, K + U], I32)
    m.scatter_idx = sb("scatter_idx", [P, K], I32)
    m.block_of = sb("block_of_step", [1, K], I32)
    m.gram = sb("gram", [D, RW])
    m.turned_gram = sb("turned_gram", [P, RW])
    m.scale_row, m.shift_row = sb("scale_row", [P, 2 * D]), sb("shift_row", [P, 2 * D])
    m.row = {n: sb(f"row_{n}", [P, D]) for n in ROWS}
    m.valid, m.twice, m.u0 = sb("valid", [P, 1]), sb("twice", [P, 1]), sb("u0", [D, 1])
    m.share = sb("share", [P, 1])
    m.rows = sb("step_rows", [P, 2, SLOTS, 2, P], I16)
    compared = sb("compared", [P, 8, P])
    m.compared = compared[:, :, :].rearrange("p q n -> p (q n)")
    m.onehot, m.same = compared[:, 0:4, :], compared[:, 4:8, :]
    wide_rows = m.rows[:, :, :, :, :].rearrange("p h s r e -> p (h s r e)").bitcast(F32)
    slots = sb("slots", [P, SLOTS * 2 * D])
    m.slot = [slots[:, i * 2 * D:(i + 1) * 2 * D] for i in range(SLOTS)]
    m.together = (m.compared[:, 0:GP * P], wide_rows[:, GP * P:2 * GP * P])
    m.turned = (wide_rows[:, 0:GP * P], slots[:, 0:GP * P])
    m.counted = (m.compared[:, 0:2 * GP * RW], slots[:, 0:2 * GP * RW])
    m.hidden_in = [m.gather_idx[:, i * SLOTS * D:(i + 1) * SLOTS * D].bitcast(F32) for i in range(2)]
    m.msg = sb("message", [P, 4, 2 * D])
    m.msg_junk = sb("junk", [P, 2, P])
    m.attr_turned = m.rows[:, :, :, :, :].rearrange("p h s r e -> p (h s r e)").bitcast(F32)[0:D, 0:SLOTS * P]
    m.hidden_out = [m.msg[:, :, :].rearrange("p r f -> p (r f)"), m.same.rearrange("p q n -> p (q n)")]
    m.zero = sb("zero", [P, RW])
    m.idx = [sb(f"idx{i}", [P, SLOTS], I32) for i in range(RUNS)]
    m.ident = sb("ident", [P, P])
    m.before = sb("before", [P, P])
    m.ones = sb("ones", [P, P])
    m.fold = sb("fold_halves", [P, P])
    m.iota_row = sb("iota_row", [P, P])
    m.part = sb("partition_no", [P, 1])
    m.trash = sb("trash_row", [P, 1])
    m.dout = sb("degree_out", [P, NB])
    m.din = sb("degree_in", [P, NB])
    m.small = sb("small", [P, 6 * D])
    m.stat = sb("stat", [P, NB])
    m.stat2 = sb("stat2", [P, NB])
    m.w = {n: sb(f"w_{n}", [P, P]) for n in WEIGHTS}
    m.w1a, m.w1a_ea = sb("w1a", [P, D]), sb("w1a_attr", [D, D])
    m.col = {n: sb(f"col_{n}", [P, 1]) for n in VECTORS}
    m.repeats = sb("repeats", [P, U])
    m.psum = [ctx.enter_context(nc.psum_tensor(f"psum{i}", [P, 512], F32)) for i in range(8)]
    m.hidden = dram("attr_products", (K // SLOTS * P, SLOTS * D))
    m.tile_keys = dram("tile_keys", (TC * P,))
    m.step_tile, m.step_block = dram("step_tile", (KC * P,), I32), dram("step_block", (KC * P,), I32)
    m.step_rows = dram("step_row_keys", (KC * P, 2 * P), I16)
    m.table = dram("node_table", (NP, D))
    m.acc = [dram(f"by_source{i}", (ACC_ROWS, RW)) for i in range(REP)]
    return m


def constants(nc, m):
    with ExitStack() as ctx:
        s = sems(nc, "iotas", "blank")
        block = ctx.enter_context(nc.Block())

        @block.gpsimd
        def _(pool):
            g = nc.gpsimd
            g.iota(m.iota_row[:, :], pattern=[[1, P]], base=0, channel_multiplier=0,
                   allow_small_or_imprecise_dtypes=True)
            g.iota(m.part[:, :], pattern=[[0, 1]], base=0, channel_multiplier=1,
                   allow_small_or_imprecise_dtypes=True)
            g.iota(m.trash[:, :], pattern=[[0, 1]], base=NP, channel_multiplier=1,
                   allow_small_or_imprecise_dtypes=True)
            pool.wait_ge(s["blank"], 4)
            g.affine_select(out=m.ident[:, :], in_=m.ident[:, :], compare_op=ALU.not_equal, fill=1.0,
                            base=0, pattern=[[-1, P]], channel_multiplier=1)
            g.affine_select(out=m.before[:, :], in_=m.ones[:, :], compare_op=ALU.is_gt, fill=0.0,
                            base=0, pattern=[[-1, P]], channel_multiplier=1)
            for shift in (-D, 0, D):
                part = g.affine_select(out=m.fold[:, :], in_=m.fold[:, :], compare_op=ALU.not_equal, fill=1.0,
                                       base=shift, pattern=[[-1, P]], channel_multiplier=1)
                part.then_inc(s["iotas"], 1)
                pool.wait_ge(s["iotas"], (shift + D) // D + 1)

        @block.vector
        def _(dve):
            v = nc.vector
            v.memset(m.ident[:, :], 0.0).then_inc(s["blank"], 1)
            v.memset(m.ones[:, :], 1.0).then_inc(s["blank"], 1)
            v.memset(m.fold[:, :], 0.0).then_inc(s["blank"], 1)
            v.memset(m.x[:, NB - 1, :], 0.0).then_inc(s["blank"], 1)
            v.memset(m.small[:, 0:CLEAR_ROWS * RW], 0.0)
            v.memset(m.h[:, :, D:RW], 1.0)


def plan_steps(nc, m, a):
    with ExitStack() as ctx:
        s = sems(nc, "numbers", "keys_in", "key", "keys_out", "keys_wide", "counted", "tiles_known", "plan_out",
                 "fetched", "placed", "loaded", "as_rows", "rows_out", "turned", "evacuated", "clear")
        sb = lambda name, shape, dt=F32: ctx.enter_context(nc.sbuf_tensor(name, shape, dt))
        keys = sb("keys", [P, TC, 1], I32)
        keyf = sb("keyf", [P, TC])
        tile_no = sb("tile_no", [P, TC])
        step_no = sb("step_no", [P, KC])
        tile_of = sb("tile_of", [P, KC])
        blk_of = sb("blk_of", [P, KC])
        tile_i = sb("tile_i", [P, KC], I32)
        blk_i = sb("blk_i", [P, KC], I32)
        wide = m.work[:, 0:NT - 1]
        junk = m.work[:, NT:2 * NT - 1]
        pair = m.both
        weights = pair[:, 2 * KC * P:3 * KC * P].rearrange("p (c e) -> p c e", c=KC)
        ends = pair[:, 0:2 * KC * P].bitcast(I32).rearrange("p (c e) -> p c e", c=KC)
        got_i = [ends[:, :, 0:P], ends[:, :, P:2 * P]]
        hh = m.h[:, :, :].rearrange("p b f -> p (b f)")
        block_i, block_f = (pair[:, i * KC * P:(i + 1) * KC * P].rearrange("p (c e) -> p c e", c=KC) for i in (4, 5))
        block_i = block_i.bitcast(I32)
        rel = pair[:, 3 * KC * P:4 * KC * P].rearrange("p (c e) -> p c e", c=KC)
        srcf = hh[:, 0:KC * P].rearrange("p (c e) -> p c e", c=KC)
        memb = hh[:, KC * P:2 * KC * P].rearrange("p (c e) -> p c e", c=KC)
        tmp = hh[:, 2 * KC * P:3 * KC * P].rearrange("p (c e) -> p c e", c=KC)
        rows16 = m.work[:, 0:KC * P].bitcast(I16).rearrange("p (c r e) -> p c r e", c=KC, r=2)
        block = ctx.enter_context(nc.Block())

        @block.gpsimd
        def _(pool):
            g = nc.gpsimd
            g.iota(tile_no[:, :], pattern=[[P, TC]], base=0, channel_multiplier=1,
                   allow_small_or_imprecise_dtypes=True).then_inc(s["numbers"], 1)
            g.iota(step_no[:, :], pattern=[[P, KC]], base=0, channel_multiplier=1,
                   allow_small_or_imprecise_dtypes=True).then_inc(s["numbers"], 1)
            pool.wait_ge(s["tiles_known"], 1)
            for c in range(KC):
                for to, table in ((ends, a["ends"]), (weights, a["edge_weight"])):
                    g.indirect_dma_start(to[:, c, :], None, table,
                                         bass.IndirectOffsetOnAxis(ap=tile_i[:, c:c + 1], axis=0)).then_inc(s["fetched"], 16)

        @block.scalar
        def _(act):
            act.wait_ge(s["rows_out"], 16)
            for acc in m.acc:
                act.dma_start(acc.rearrange("(p r c) f -> p r (c f)", p=P, c=CLEAR_ROWS),
                              m.small[:, 0:CLEAR_ROWS * RW].unsqueeze(1)
                              .to_broadcast([P, ACC_ROWS // P // CLEAR_ROWS, CLEAR_ROWS * RW])).then_inc(m.cleared, 16)

        @block.sync
        def _(sp):
            sp.dma_start(keys[:, :, :], a["ends"].rearrange("(c p) e -> p c e", p=P)[:, :, 2 * P - 1:2 * P],
                         allow_slow_non_contiguous=True).then_inc(s["keys_in"], 16)
            sp.wait_ge(s["key"], 3)
            sp.dma_start(m.tile_keys.rearrange("(c p) -> p c", p=P), keyf[:, :],
                         allow_slow_non_contiguous=True).then_inc(s["keys_out"], 16)
            sp.wait_ge(s["keys_out"], 16)
            sp.dma_start(wide, m.tile_keys[0:NT - 1].partition_broadcast(P)).then_inc(s["keys_wide"], 16)
            sp.dma_start(m.x[:, 0:NB - 1, :], node_rows(a["x"], 0, NB - 1)).then_inc(s["loaded"], 16)
            sp.dma_start(m.x[0:LAST, NB - 1, :], a["x"][(NB - 1) * P:N, :]).then_inc(s["loaded"], 16)
            sp.wait_ge(s["tiles_known"], 2)
            for to, frm in ((m.step_tile, tile_i), (m.step_block, blk_i)):
                sp.dma_start(to.rearrange("(c p) -> p c", p=P), frm[:, :],
                             allow_slow_non_contiguous=True).then_inc(s["plan_out"], 16)
            sp.wait_ge(s["plan_out"], 32)
            sp.dma_start(m.block_of[:, :], m.step_block[0:K].rearrange("(a k) -> a k", a=1)).then_inc(s["plan_out"], 16)
            sp.wait_ge(s["as_rows"], 3)
            sp.dma_start(m.step_rows.rearrange("(c p) e -> p c e", p=P),
                         rows16.rearrange("p c r e -> p c (r e)")).then_inc(s["rows_out"], 16)
            sp.wait_ge(s["rows_out"], 16)
            sp.wait_ge(s["plan_out"], 48)
            sp.wait_ge(s["loaded"], 32)

        @block.vector
        def _(dve):
            v = nc.vector
            dve.wait_ge(s["keys_in"], 16)
            v.tensor_scalar(keys[:, :, 0], keys[:, :, 0], 7, None, ALU.arith_shift_right).then_inc(s["key"], 1)
            dve.wait_ge(s["key"], 1)
            v.tensor_copy(keyf[:, :], keys[:, :, 0]).then_inc(s["key"], 1)
            dve.wait_ge(s["key"], 2)
            dve.wait_ge(s["numbers"], 2)
            v.tensor_tensor(keyf[:, :], keyf[:, :], tile_no[:, :], ALU.add).then_inc(s["key"], 1)
            dve.wait_ge(s["keys_wide"], 16)
            for c in range(KC):
                v.tensor_scalar(junk, wide, step_no[:, c:c + 1], 0.0, ALU.is_lt, ALU.add,
                                accum_out=tile_of[:, c:c + 1]).then_inc(s["counted"], 1)
                dve.wait_ge(s["counted"], c + 1)
            v.tensor_tensor(blk_of[:, :], step_no[:, :], tile_of[:, :], ALU.subtract).then_inc(s["clear"], 1)
            v.tensor_copy(tile_i[:, :], tile_of[:, :]).then_inc(s["tiles_known"], 1)
            dve.wait_ge(s["clear"], 1)
            v.tensor_scalar(blk_i[:, :], blk_of[:, :], float(NB - 1), None, ALU.min).then_inc(s["tiles_known"], 1)
            v.tensor_scalar(blk_of[:, :], blk_of[:, :], -float(P), None, ALU.mult).then_inc(s["clear"], 1)
            dve.wait_ge(s["fetched"], 16 * 2 * KC)
            dve.wait_ge(s["clear"], 2)
            v.tensor_scalar(block_i, got_i[0], 7, None, ALU.arith_shift_right).then_inc(s["placed"], 1)
            v.tensor_copy(srcf, got_i[0]).then_inc(s["placed"], 1)
            dve.wait_ge(s["placed"], 2)
            v.tensor_copy(block_f, block_i).then_inc(s["placed"], 1)
            v.tensor_scalar(srcf, srcf, float(NB), None, ALU.mult).then_inc(s["placed"], 1)
            dve.wait_ge(s["placed"], 4)
            v.scalar_tensor_tensor(srcf, block_f, float(1 - P * NB), srcf, ALU.mult, ALU.add).then_inc(s["as_rows"], 1)
            v.tensor_copy(rel, got_i[1]).then_inc(s["clear"], 1)
            dve.wait_ge(s["as_rows"], 1)
            v.tensor_copy(rows16[:, :, 1, :], srcf).then_inc(s["as_rows"], 1)
            dve.wait_ge(s["clear"], 3)
            v.tensor_scalar(tmp, rel, float(N), None, ALU.is_lt).then_inc(s["clear"], 1)
            dve.wait_ge(s["clear"], 4)
            for c in range(KC):
                v.tensor_scalar(rel[:, c, :], rel[:, c, :], blk_of[:, c:c + 1], None, ALU.add).then_inc(s["clear"], 1)
            dve.wait_ge(s["clear"], 4 + KC)
            v.tensor_copy(rows16[:, :, 0, :], rel).then_inc(s["as_rows"], 1)
            v.tensor_scalar(memb, rel, 0.0, None, ALU.is_ge).then_inc(s["clear"], 1)
            dve.wait_ge(s["clear"], 5 + KC)
            v.tensor_tensor(memb, memb, tmp, ALU.mult).then_inc(s["clear"], 1)
            dve.wait_ge(s["clear"], 6 + KC)
            v.tensor_scalar(tmp, rel, float(P), None, ALU.is_lt).then_inc(s["clear"], 1)
            dve.wait_ge(s["clear"], 7 + KC)
            v.tensor_tensor(memb, memb, tmp, ALU.mult).then_inc(s["clear"], 1)
            for c in range(KC):
                n = min(P, K - c * P)
                dve.wait_ge(s["turned"], c + 1)
                v.tensor_copy(m.cols[:, :, c * P:c * P + n],
                              m.psum[c % 2][:, :].rearrange("p (a k) -> p a k", a=4)[:, :, 0:n]).then_inc(s["evacuated"], 1)
            dve.wait_ge(s["evacuated"], KC)
            v.tensor_copy(m.gather_idx[:, 0:K], m.src).then_inc(s["evacuated"], 1)

        @block.tensor
        def _(pe):
            pe.wait_ge(s["as_rows"], 3)
            pe.wait_ge(s["clear"], 8 + KC)
            for c in range(KC):
                if c >= 2:
                    pe.wait_ge(s["evacuated"], c - 1)
                for i, frm in enumerate((srcf, rel, weights, memb)):
                    last = nc.tensor.transpose(m.psum[c % 2][:, i * P:(i + 1) * P], frm[:, c, :], m.ident[:, :])
                last.then_inc(s["turned"], 1)


def layer_norm(nc, m):
    with ExitStack() as ctx:
        s = sems(nc, "mean", "centred", "square", "variance", "rooted")
        centred = m.work[:, 0:NB * D].rearrange("p (b f) -> p b f", b=NB)
        h = m.h[:, :, 0:D]
        halves = (slice(0, NB // 2), slice(NB // 2, NB))
        wide = lambda t: t.unsqueeze(2).to_broadcast([P, NB // 2, D])
        block = ctx.enter_context(nc.Block())

        @block.vector
        def _(dve):
            v = nc.vector
            for n, part in enumerate(halves):
                v.tensor_reduce(m.stat[:, part], m.x[:, part, :], AX, ALU.add).then_inc(s["mean"], 1)
                dve.wait_ge(s["mean"], 2 * n + 1)
                v.tensor_scalar(m.stat[:, part], m.stat[:, part], -1.0 / D, None, ALU.mult).then_inc(s["mean"], 1)
                dve.wait_ge(s["mean"], 2 * n + 2)
                v.tensor_tensor(centred[:, part, :], m.x[:, part, :], wide(m.stat[:, part]), ALU.add).then_inc(s["centred"], 1)
            for n, part in enumerate(halves):
                dve.wait_ge(s["square"], n + 1)
                v.tensor_reduce(m.stat2[:, part], h[:, part, :], AX, ALU.add).then_inc(s["variance"], 1)
                dve.wait_ge(s["variance"], 2 * n + 1)
                v.tensor_scalar(m.stat2[:, part], m.stat2[:, part], 1.0 / D, EPS, ALU.mult, ALU.add).then_inc(s["variance"], 1)
            for n, part in enumerate(halves):
                dve.wait_ge(s["rooted"], n + 1)
                v.reciprocal(m.stat2[:, part], m.stat[:, part]).then_inc(s["variance"], 1)
                dve.wait_ge(s["variance"], 5 + n)
                v.scalar_tensor_tensor(h[:, part, :], centred[:, part, :], 0.0, wide(m.stat2[:, part]), ALU.max, ALU.mult)

        @block.scalar
        def _(act):
            for n, part in enumerate(halves):
                act.wait_ge(s["centred"], n + 1)
                nc.scalar.activation(h[:, part, :], centred[:, part, :], ACT.Square).then_inc(s["square"], 1)
            for n, part in enumerate(halves):
                act.wait_ge(s["variance"], 2 * n + 2)
                nc.scalar.activation(m.stat[:, part], m.stat2[:, part], ACT.Sqrt).then_inc(s["rooted"], 1)


BANKS = ((0, 4), (4, GP))


def group_of(array, group, lo=0, hi=GP, width=D):
    stride = array.shape[2]
    flat = array.rearrange("p b f -> p (b f)")
    part = flat[:, bass.ds(group * (GP * 2 * stride) + lo * 2 * stride, (hi - lo) * 2 * stride)]
    return part.rearrange("p (b f) -> p b f", f=stride)[:, :, 0:width]


def after(u, n=0):
    return u * 2 + 4 + n


def two_before(u):
    return u * 2 + 2


def in_pairs(engine, units, body, lead=None):
    pairs = units // 2 if lead is None else (units - 1) // 2
    if lead is not None:
        lead(0, 0)
    with engine.Fori(0, pairs) as i:
        for n in range(2):
            if lead is not None:
                lead(i, n + 1)
            body(i, n)
    for u in range(2 * pairs, units):
        if lead is not None and u + 1 < units:
            lead(u // 2, u % 2 + 1)
        body(u // 2, u % 2)


def bring(nc, pool, sources, group, to):
    rows = to.rearrange("p (b f) -> p b f", f=D)
    if len(sources) == 1:
        return nc.gpsimd.tensor_copy(rows, group_of(sources[0], group))
    return nc.gpsimd.tensor_tensor(rows, group_of(sources[0], group), group_of(sources[1], group), ALU.add)


def node_product(nc, m, sources, weight, put, row=None):
    with ExitStack() as ctx:
        s = sems(nc, "brought", "turned", "columns", "product", "put")
        block = ctx.enter_context(nc.Block())

        @block.gpsimd
        def _(pool):
            def body(i, n):
                g = 2 * i + n
                pool.wait_ge(s["turned"], two_before(g))
                settle(pool)
                bring(nc, pool, sources, g, m.together[n]).then_inc(s["brought"], 1)

            pool.sem_inc(s["turned"], 4)
            in_pairs(pool, GROUPS, body)

        @block.tensor
        def _(pe):
            def turn(i, n):
                g = 2 * i + n
                pe.wait_ge(s["columns"], two_before(g))
                pe.wait_ge(s["brought"], g + 1)
                for b, (lo, hi) in enumerate(BANKS):
                    for q in range(lo, hi):
                        last = nc.tensor.transpose(m.psum[n % 2 * 2 + b][:, (q - lo) * P:(q - lo + 1) * P],
                                                   m.together[n % 2][:, q * P:(q + 1) * P], m.ident[:, :])
                    last.then_inc(s["turned"], 1)

            def multiply(i, n):
                g = 2 * i + n
                pe.wait_ge(s["put"], two_before(g))
                for b, (lo, hi) in enumerate(BANKS):
                    pe.wait_ge(s["columns"], after(g, b + 1))
                    for q in range(lo, hi):
                        to = m.psum[4 + n * 2 + b][:, (q - lo) * P:(q - lo + 1) * P]
                        last = nc.tensor.matmul(to, m.turned[n][:, q * P:(q + 1) * P], weight[:, :],
                                                start=True, stop=row is None)
                        if row is not None:
                            last = nc.tensor.matmul(to, m.ones[0:1, :], row[0:1, :], start=False, stop=True)
                    last.then_inc(s["product"], 1)

            pe.sem_inc(s["columns"], 4)
            pe.sem_inc(s["put"], 4)
            in_pairs(pe, GROUPS, multiply, lead=turn)

        @block.scalar
        def _(act):
            def body(i, n):
                g = 2 * i + n
                act.wait_ge(s["product"], two_before(g))
                for b, (lo, hi) in enumerate(BANKS):
                    act.wait_ge(s["turned"], after(g, b + 1))
                    nc.scalar.activation(m.turned[n][:, lo * P:hi * P], m.psum[n * 2 + b][:, 0:(hi - lo) * P],
                                         ACT.Copy).then_inc(s["columns"], 1)

            act.sem_inc(s["product"], 4)
            in_pairs(act, GROUPS, body)

        @block.vector
        def _(dve):
            def body(i, n):
                g = 2 * i + n
                for b, (lo, hi) in enumerate(BANKS):
                    dve.wait_ge(s["product"], after(g, b + 1))
                    put(g, lo, hi, m.psum[4 + n * 2 + b][:, 0:(hi - lo) * P]
                        .rearrange("p (b f) -> p b f", f=D)).then_inc(s["put"], 1)

            in_pairs(dve, GROUPS, body)


def put_rows(nc, to):
    return lambda g, lo, hi, rows: nc.vector.tensor_copy(group_of(to, g, lo, hi), rows)


def settle(engine):
    engine.nop(nofuse=True)


def run_values(nc, engine, ap, most):
    _, values = nc.values_load_multi_w_load_instructions(
        ap, engines=(engine,), min_val=0, max_val=most, skip_runtime_bounds_check_because="the plan bounds them")
    return values


def ahead(k, n):
    return k + 1 + n


def steps_by_source(nc, m, last_layer):
    with ExitStack() as ctx:
        s = sems(nc, "onehot", "same", "z", "msg", "summed", "staged", "idx", "repeat", "fix",
                 "scaled", "sum", "began", "gram_done", "junk_clear")
        rows_in = ring(nc, "rows_in", 2)
        scattered = ring(nc, "scattered", SLOTS)
        hidden_in = ring(nc, "hidden_in", 2)
        block = ctx.enter_context(nc.Block())
        H = SLOTS
        R = 4
        B = 4
        SB = 2 if last_layer else 4
        GRAM = 6

        def products(j, steps=1):
            return m.hidden_in[j // H % 2][:, j % H * D:(j % H + steps) * D]

        @block.sync
        def _(sp):
            keys = m.step_rows.rearrange("k e -> (k e)")
            sp.wait_ge(s["began"], 1)
            if not last_layer:
                sp.wait_ge(m.cleared, 16 * REP)
            with sp.Fori(0, IT) as i:
                for run in range(RUNS):
                    sp.wait_ge(s["same"] if last_layer else s["repeat"], ahead(i * U + run * H + H - 1 - 2 * H, U))
                    sp.dma_start(m.rows[:, run % 2].rearrange("p s r e -> p (s r e)"),
                                 keys[bass.ds(i * (U * 2 * P) + run * (H * 2 * P), H * 2 * P)].partition_broadcast(P)
                                 ).then_inc(rows_in[run % 2], 16)
                    if last_layer:
                        sp.wait_ge(s["msg"], ahead(i * U + run * H + H - 1 - 2 * H, U))
                        sp.dma_start(m.hidden_in[run % 2], m.hidden[bass.ds((i * RUNS + run) * P, P), :]
                                     ).then_inc(hidden_in[run % 2], 16)

        @block.vector
        def _(dve):
            v = nc.vector
            v.memset(m.msg[:, :, D:RW], 1.0).then_inc(s["junk_clear"], 1)
            v.memset(m.zero[:, :], 0.0).then_inc(s["junk_clear"], 1)
            dve.wait_ge(s["began"], 1)
            v.sem_inc(s["idx"], 1)

            def add_row(i, j):
                k = i * U + j
                dve.wait_ge(s["z"], ahead(k, R))
                dve.wait_ge(s["scaled"], i * (U // R) + j // R + 1)
                v.tensor_tensor(products(j), products(j), m.psum[j % B][:, 0:D], ALU.add).then_inc(s["sum"], 1)

            def steps(i, first=False):
                def compare(j):
                    k = i * U + j
                    run, n = divmod(j, H)
                    if n == 0:
                        dve.wait_ge(rows_in[run % 2], i * (8 * RUNS) + run // 2 * 16 + 16)
                    rel_row, src_row = m.rows[:, run % 2, n, 0, :], m.rows[:, run % 2, n, 1, :]
                    src_col = m.src[:, bass.ds(k, 1)]
                    dve.wait_ge(s["z"], ahead(k - R, R))
                    v.tensor_scalar(m.onehot[:, j % R, :], rel_row, m.part[:, :], None, ALU.is_equal).then_inc(s["onehot"], 1)
                    dve.wait_ge(s["summed"], ahead(k - R, R))
                    v.tensor_scalar(m.same[:, j % R, :], src_row, src_col, None, ALU.is_equal).then_inc(s["same"], 1)
                    if last_layer:
                        return
                    dve.wait_ge(s["repeat"], ahead(k - 2, U))
                    v.scalar_tensor_tensor(m.msg_junk[:, j % 2, :], src_row, src_col, m.before[:, :], ALU.is_equal, ALU.mult,
                                           accum_out=m.repeats[:, j:j + 1]).then_inc(s["repeat"], 1)

                def aim(run):
                    k = i * U + run * H
                    at = m.scatter_idx[:, bass.ds(k, H)]
                    if last_layer:
                        dve.wait_ge(s["staged"], ahead(k - U + 2 * H - 1, U))
                        v.tensor_copy(m.idx[run][:, :], at).then_inc(s["idx"], 1)
                        return
                    dve.wait_ge(s["repeat"], ahead(k + H - 1, U))
                    f = i * (4 * RUNS) + run * 4
                    rep, src = m.repeats[:, run * H:run * H + H], m.src[:, bass.ds(k, H)]
                    to_trash = m.small[:, 0:H]
                    dve.wait_ge(s["idx"], i * RUNS + run + 1)
                    v.tensor_scalar(rep, rep, 0.0, None, ALU.is_gt).then_inc(s["fix"], 1)
                    v.tensor_scalar(to_trash, src, -1.0, m.trash[:, :], ALU.mult, ALU.add).then_inc(s["fix"], 1)
                    dve.wait_ge(s["fix"], f + 2)
                    v.tensor_tensor(to_trash, to_trash, rep, ALU.mult).then_inc(s["fix"], 1)
                    dve.wait_ge(s["fix"], f + 3)
                    v.tensor_tensor(at, to_trash, src, ALU.add).then_inc(s["fix"], 1)
                    dve.wait_ge(s["staged"], ahead(k - U + 2 * H - 1, U))
                    v.tensor_tensor(m.idx[run][:, :], to_trash, src, ALU.add).then_inc(s["idx"], 1)

                def scale(j):
                    if j % H == 0:
                        dve.wait_ge(hidden_in[j // H % 2], i * (8 * RUNS) + j // H // 2 * 16 + 16)
                    part = products(j, R).rearrange("p (k f) -> p k f", f=D)
                    v.tensor_tensor(part, part, m.scale_row[:, 0:D].unsqueeze(1).to_broadcast([P, R, D]),
                                    ALU.mult).then_inc(s["scaled"], 1)

                for j in range(U):
                    compare(j)
                    if last_layer and not (first and j == 0):
                        add_row(i, j - 1)
                    if last_layer and j % R == 0:
                        scale(j)
                    if j % H == H - 1:
                        aim(j // H)

            steps(0, first=True)
            with dve.Fori(1, IT) as i:
                steps(i)
            if last_layer:
                add_row(IT, -1)

        @block.tensor
        def _(pe):
            pe.wait_ge(s["junk_clear"], 2)
            pe.sem_inc(s["z"], R)
            pe.sem_inc(s["same"], U)
            pe.sem_inc(s["repeat"], U)
            pe.sem_inc(s["staged"], U)
            pe.sem_inc(s["summed"], R)
            pe.sem_inc(s["msg"], U)
            if last_layer:
                nc.tensor.matmul(m.psum[GRAM][0:D, 0:RW], m.zero[:, 0:D], m.zero[:, 0:RW], start=True, stop=False,
                                 skip_group_check=True)
                pe.sem_inc(s["sum"], B)
            pe.sem_inc(s["began"], 1)

            def sum_same(i, j):
                k = i * U + j
                pe.wait_ge(s["same"], ahead(k, U))
                pe.wait_ge(s["msg"], ahead(k, U))
                pe.wait_ge(s["staged"], ahead(k - SB, U))
                if last_layer:
                    nc.tensor.matmul(m.psum[GRAM][0:D, 0:RW], m.msg[:, j % R, 0:D], m.msg[:, j % R, 0:RW],
                                     start=False, stop=False, skip_group_check=True)
                nc.tensor.matmul(m.psum[B + j % SB][:, 0:RW], m.same[:, j % R, :], m.msg[:, j % R, 0:RW],
                                 start=True, stop=True).then_inc(s["summed"], 1)

            def steps(i, first=False):
                blocks = []

                def expand(j):
                    k = i * U + j
                    pe.wait_ge(s["onehot"], k + 1)
                    if last_layer:
                        pe.wait_ge(s["sum"], ahead(k - B, B))
                    else:
                        pe.wait_ge(s["msg"], ahead(k - B, U))
                    nc.tensor.matmul(m.psum[j % B][:, 0:D], m.onehot[:, j % R, :],
                                     m.both[:, bass.ds(blocks[j] * (2 * D), D)], start=True, stop=True).then_inc(s["z"], 1)

                for j in range(U):
                    if j % H == 0:
                        blocks += run_values(nc, ENG.PE, m.block_of[0:1, bass.ds(i * U + j, H)], NB - 1)
                    expand(j)
                    if not first or j >= 2:
                        sum_same(i, j - 2)

            steps(0, first=True)
            with pe.Fori(1, IT) as i:
                steps(i)
            sum_same(IT, -2)
            sum_same(IT, -1)
            if last_layer:
                nc.tensor.matmul(m.psum[GRAM][0:D, 0:RW], m.zero[:, 0:D], m.zero[:, 0:RW], start=False, stop=True,
                                 skip_group_check=True).then_inc(s["gram_done"], 1)

        @block.scalar
        def _(act):
            a = nc.scalar
            act.wait_ge(s["began"], 1)

            def stage(i, j, first=False):
                act.wait_ge(s["summed"], ahead(i * U + j, R))
                if not first or j >= H:
                    act.wait_ge(scattered[j % H], i * (16 * RUNS) + (j // H) * 16)
                a.activation(m.slot[j % H][:, 0:RW], m.psum[B + j % SB][:, 0:RW], ACT.Copy).then_inc(s["staged"], 1)

            def steps(i, first=False):
                def weigh(j):
                    k = i * U + j
                    act.wait_ge(s["summed"], ahead(k - R, R))
                    msg, z = m.msg[:, j % R, 0:D], m.psum[j % B][:, 0:D]
                    if last_layer:
                        act.wait_ge(s["sum"], ahead(k, B))
                        a.activation(msg, products(j), ACT.Relu).then_inc(s["msg"], 1)
                    else:
                        act.wait_ge(s["z"], ahead(k, R))
                        settle(act)
                        a.activation(m.msg[:, j % R, D:RW], m.member[:, bass.ds(k, 1)], ACT.Copy)
                        a.activation(msg, z, ACT.Copy, scale=m.wt[:, bass.ds(k, 1)]).then_inc(s["msg"], 1)

                for j in range(U):
                    weigh(j)
                    if not first or j >= 2:
                        stage(i, j - 2, first)

            steps(0, first=True)
            with act.Fori(1, IT) as i:
                steps(i)
            stage(IT, -2)
            stage(IT, -1)
            if last_layer:
                act.wait_ge(s["gram_done"], 1)
                a.activation(m.gram[:, :], m.psum[GRAM][0:D, 0:RW], ACT.Copy)

        @block.gpsimd
        def _(pool):
            pool.wait_ge(s["began"], 1)
            with pool.Fori(0, IT) as i:
                for j in range(U):
                    if j % H == 0:
                        pool.wait_ge(s["idx"], i * RUNS + j // H + 2)
                    pool.wait_ge(s["staged"], ahead(i * U + j, U))
                    settle(pool)
                    nc.gpsimd.indirect_dma_start(m.acc[j % REP],
                                                 bass.IndirectOffsetOnAxis(ap=m.idx[j // H][:, j % H:j % H + 1], axis=0),
                                                 m.slot[j % H][:, 0:RW], None, compute_op=ALU.add).then_inc(scattered[j % H], 16)
            for n in range(SLOTS):
                pool.wait_ge(scattered[n], IT * 16 * RUNS)


def steps_by_target(nc, m, inputs, with_attr):
    with ExitStack() as ctx:
        s = sems(nc, "onehot", "summed", "added", "idx", "message", "marked", "sum", "clear", "began", "gram_done",
                 "blank", "cleared", "projected", "held")
        gathered = ring(nc, "gathered", SLOTS)
        attr_in = ring(nc, "attr_in", SLOTS)
        hidden_out = ring(nc, "hidden_out", 2)
        block = ctx.enter_context(nc.Block())
        H, R, GRAM, HIDDEN = SLOTS, 4, 4, 4
        width = 2 * D if with_attr else RW
        clears = 2 if with_attr else 2 + SLOTS

        @block.sync
        def _(sp):
            sp.wait_ge(s["began"], 1)
            with sp.Fori(0, IT) as i:
                for run in range(RUNS):
                    tiles = run_values(nc, ENG.SP, m.step_tile[bass.ds(i * U + run * H, H)].rearrange("(a k) -> a k", a=1), NT - 1)
                    for n in range(H):
                        k = i * U + run * H + n
                        if with_attr:
                            sp.wait_ge(s["summed"], ahead(k - SLOTS, SLOTS))
                            sp.dma_start(m.slot[n][:, D:2 * D], inputs["edge_attr"][bass.ds(tiles[n] * P, P), :]
                                         ).then_inc(attr_in[n], 16)
                        else:
                            sp.wait_ge(s["projected"], ahead(k - SLOTS, SLOTS))
                            sp.dma_start(m.attr_turned[:, n * P:(n + 1) * P],
                                         inputs["attr_turned"][bass.ds(tiles[n] * D, D), :]).then_inc(attr_in[n], 16)

        @block.vector
        def _(dve):
            v = nc.vector
            v.memset(m.zero[:, :], 0.0).then_inc(s["clear"], 1)
            v.memset(m.gather_idx[:, K:K + U], 0).then_inc(s["clear"], 1)
            if not with_attr:
                for slot in m.slot:
                    v.memset(slot[:, D:RW], 1.0).then_inc(s["clear"], 1)
            dve.wait_ge(s["clear"], clears)
            for run in range(RUNS):
                v.tensor_copy(m.idx[run][:, :], m.gather_idx[:, run * H:run * H + H]).then_inc(s["idx"], 1)
            dve.wait_ge(s["began"], 1)
            v.sem_inc(s["added"], R)
            dve.wait_ge(s["blank"], 1)

            def match(i, j):
                k = i * U + j
                dve.wait_ge(s["summed"], ahead(k - R, SLOTS))
                v.tensor_scalar(m.onehot[:, j % R, :], m.iota_row[:, :], m.rel[:, bass.ds(k, 1)], None,
                                ALU.is_equal).then_inc(s["onehot"], 1)

            def steps(i, last=False):
                blocks = []

                def add_attr(j):
                    dve.wait_ge(gathered[j % H], i * (16 * RUNS) + (j // H) * 16 + 16)
                    dve.wait_ge(attr_in[j % H], i * (16 * RUNS) + (j // H) * 16 + 16)
                    slot = m.slot[j % H]
                    v.tensor_tensor(slot[:, 0:D], slot[:, 0:D], slot[:, D:2 * D], ALU.add).then_inc(s["sum"], 1)

                def add_block(j):
                    k = i * U + j
                    dve.wait_ge(s["summed"], ahead(k, SLOTS))
                    dve.wait_ge(s["added"], ahead(k - 1, R))
                    rows = m.both[:, bass.ds(blocks[j] * (2 * D), width)]
                    v.tensor_tensor(rows, rows, m.psum[j % R][:, 0:width], ALU.add).then_inc(s["added"], 1)

                for j in range(U + 2):
                    if j < U and not (last and j >= U - 2):
                        match(i, j + 2)
                    if j < U and with_attr:
                        add_attr(j)
                    if j < U and j % H == 0:
                        blocks += run_values(nc, ENG.DVE, m.block_of[0:1, bass.ds(i * U + j, H)], NB - 1)
                    if j >= 2:
                        add_block(j - 2)
                    if j >= H and (j - 1) % H == 0:
                        run = j // H - 1
                        v.tensor_copy(m.idx[run][:, :], m.gather_idx[:, bass.ds(i * U + U + run * H, H)]).then_inc(s["idx"], 1)

            match(0, 0)
            match(0, 1)
            with dve.Fori(0, IT - 1) as i:
                steps(i)
            steps(IT - 1, last=True)

        @block.tensor
        def _(pe):
            pe.wait_ge(s["clear"], clears)
            pe.sem_inc(s["summed"], SLOTS)
            pe.sem_inc(s["projected"], SLOTS)
            pe.sem_inc(s["held"], R)
            if with_attr:
                nc.tensor.matmul(m.psum[GRAM][0:D, 0:D], m.zero[:, 0:D], m.zero[:, 0:D], start=True, stop=False,
                                 skip_group_check=True)
            pe.sem_inc(s["began"], 1)
            with pe.Fori(0, IT) as i:
                for j in range(U):
                    k = i * U + j
                    rows = m.slot[j % H]
                    if not with_attr:
                        pe.wait_ge(s["held"], ahead(k - R, R))
                        pe.wait_ge(attr_in[j % H], i * (16 * RUNS) + (j // H) * 16 + 16)
                        nc.tensor.matmul(m.psum[HIDDEN + j % R][:, 0:D], m.attr_turned[:, j % H * P:(j % H + 1) * P],
                                         m.w1a_ea[:, :], start=True, stop=True).then_inc(s["projected"], 1)
                    pe.wait_ge(s["onehot"], k + 1)
                    pe.wait_ge(s["added"], ahead(k - R, R))
                    if with_attr:
                        pe.wait_ge(s["marked"], k + 1)
                        nc.tensor.matmul(m.psum[GRAM][0:D, 0:D], m.msg[:, j % R, 0:D], rows[:, D:2 * D],
                                         start=False, stop=False, skip_group_check=True)
                        pe.wait_ge(s["message"], k + 1)
                    else:
                        pe.wait_ge(gathered[j % H], i * (16 * RUNS) + (j // H) * 16 + 16)
                    nc.tensor.matmul(m.psum[j % R][:, 0:width], m.onehot[:, j % R, :], rows[:, 0:width],
                                     start=True, stop=True).then_inc(s["summed"], 1)
            if with_attr:
                nc.tensor.matmul(m.psum[GRAM][0:D, 0:D], m.zero[:, 0:D], m.zero[:, 0:D], start=False, stop=True,
                                 skip_group_check=True).then_inc(s["gram_done"], 1)

        @block.scalar
        def _(act):
            a = nc.scalar
            act.wait_ge(s["clear"], clears)
            a.activation(m.pair[:, :, 0:width], m.zero[:, 0:1].unsqueeze(2).to_broadcast([P, NB, width]),
                         ACT.Copy).then_inc(s["blank"], 1)
            if not with_attr:
                a.activation(m.work[:, 0:PIECE], m.zero[:, 0:1].to_broadcast([P, PIECE]), ACT.Copy).then_inc(s["blank"], 1)
                act.wait_ge(s["blank"], 2)
            act.wait_ge(s["began"], 1)

            def message_steps(i):
                for j in range(U):
                    k = i * U + j
                    slot = m.slot[j % H]
                    act.wait_ge(s["summed"], ahead(k - R, SLOTS))
                    act.wait_ge(attr_in[j % H], i * (16 * RUNS) + (j // H) * 16 + 16)
                    settle(act)
                    a.activation(m.msg[:, j % R, 0:D], slot[:, D:2 * D], ACT.Copy,
                                 scale=m.member[:, bass.ds(k, 1)]).then_inc(s["marked"], 1)
                    act.wait_ge(s["sum"], k + 1)
                    a.activation(slot[:, 0:D], slot[:, 0:D], ACT.Relu).then_inc(s["message"], 1)

            def product_steps(i, first=False):
                for run in range(RUNS):
                    if not first or run >= 2:
                        act.wait_ge(hidden_out[run % 2], i * (8 * RUNS) + run // 2 * 16)
                    for n in range(H):
                        k = i * U + run * H + n
                        act.wait_ge(s["projected"], ahead(k, SLOTS))
                        settle(act)
                        a.activation(m.hidden_out[run % 2][:, n * D:(n + 1) * D], m.psum[HIDDEN + n % R][:, 0:D], ACT.Copy,
                                     scale=m.member[:, bass.ds(k, 1)]).then_inc(s["held"], 1)
                    act.wait_ge(s["held"], ahead(i * U + run * H + H - 1, R))
                    act.dma_start(m.hidden[bass.ds((i * RUNS + run) * P, P), :], m.hidden_out[run % 2]
                                  ).then_inc(hidden_out[run % 2], 16)
                    for acc in m.acc[run * REP // RUNS:(run + 1) * REP // RUNS]:
                        act.dma_start(acc.rearrange("a f -> (a f)")[bass.ds(i * (P * PIECE), P * PIECE)]
                                      .rearrange("(p r) -> p r", p=P), m.work[:, 0:PIECE]).then_inc(s["cleared"], 16)

            if with_attr:
                with act.Fori(0, IT) as i:
                    message_steps(i)
                act.wait_ge(s["gram_done"], 1)
                a.activation(m.gram[:, 0:D], m.psum[GRAM][0:D, 0:D], ACT.Copy)
            else:
                product_steps(0, first=True)
                with act.Fori(1, IT) as i:
                    product_steps(i)
                for done in hidden_out:
                    act.wait_ge(done, IT * 8 * RUNS)
                act.wait_ge(s["cleared"], 16 * IT * REP)

        @block.gpsimd
        def _(pool):
            pool.wait_ge(s["began"], 1)
            with pool.Fori(0, IT) as i:
                for j in range(U):
                    if j % H == 0:
                        pool.wait_ge(s["idx"], i * RUNS + j // H + 1)
                    pool.wait_ge(s["summed"], ahead(i * U + j - SLOTS, SLOTS))
                    settle(pool)
                    nc.gpsimd.indirect_dma_start(m.slot[j % H][:, 0:D], None, m.table,
                                                 bass.IndirectOffsetOnAxis(ap=m.idx[j // H][:, j % H:j % H + 1], axis=0)
                                                 ).then_inc(gathered[j % H], 16)


def load_parameters(nc, m, a):
    with ExitStack() as ctx:
        s = sems(nc, "blank", "loaded", "u_done")
        block = ctx.enter_context(nc.Block())
        squares = {"hamilton": a["hamilton"], "l1": a["l1_w"], "l2a": a["l2_w1"], "l2b": a["l2_w2"], "l3_h": a["w1a"][0:D, :],
                   "l3_b": a["w1b"], "l3_x": a["w2a"][0:D, :], "l3_agg": a["w2a"][D:2 * D, :], "l3_out": a["w2b"]}
        columns = {"gamma": a["gamma"], "beta": a["beta"], "l2_b1": a["l2_b1"], "l2_b2": a["l2_b2"], "g2a": a["g2a"], "b2a": a["b2a"],
                   "g2b": a["g2b"], "b2b": a["b2b"]}
        rows = {"l1_bias": a["l1_bias"], "g1a": a["g1a"], "b1a": a["b1a"], "g1b": a["g1b"], "b1b": a["b1b"]}
        signs, wu = m.work[:, 0:P], m.work[0:D, P:2 * P]
        s_loads = 2 * len(squares) + 2 + 2 * len(columns) + len(rows) + 2 + 3

        @block.vector
        def _(dve):
            v = nc.vector
            for w in m.w.values():
                v.memset(w[:, :], 0.0).then_inc(s["blank"], 1)
            v.memset(signs, 0.0).then_inc(s["blank"], 1)
            v.memset(m.valid[:, :], 1.0)
            v.memset(m.twice[0:D, :], 1.0)
            v.memset(m.twice[D:P, :], 2.0)
            v.memset(m.share[0:D, :], Q * P / N)
            v.memset(m.share[D:P, :], (N - Q * P) / N)
            dve.wait_ge(s["loaded"], 16 * s_loads)
            v.tensor_tensor(m.w["hamilton"][:, :], m.w["hamilton"][:, :], signs, ALU.mult)
            dve.wait_ge(s["u_done"], 1)
            v.tensor_copy(m.col["l3_u"][:, :], m.psum[0][:, 0:1])

        @block.sync
        def _(sp):
            n = 0

            def load(to, frm):
                sp.dma_start(to, frm).then_inc(s["loaded"], 16)
                return 1

            column = lambda t: t.rearrange("(p a) -> p a", a=1)
            for name, frm in columns.items():
                n += load(m.col[name][0:D, :], column(frm)) + load(m.col[name][D:P, :], column(frm))
            for name, frm in rows.items():
                n += load(m.row[name][:, :], frm.partition_broadcast(P))
            n += load(m.w1a[:, :], a["w1a"]) + load(m.w1a_ea[:, :], a["w1a"][D:2 * D, :])
            n += load(wu[:, 0:D], a["w2a"][2 * D:3 * D, :]) + load(wu[:, D:P], a["w2a"][2 * D:3 * D, :])
            n += load(m.u0[:, :], column(a["u"][0, :]))
            sp.wait_ge(s["blank"], len(WEIGHTS) + 1)
            for name, frm in squares.items():
                n += load(m.w[name][0:D, 0:D], frm) + load(m.w[name][D:P, D:P], frm)
            n += load(signs[0:D, 0:D], a["signs"]) + load(signs[D:P, D:P], a["signs"])
            assert n == s_loads, (n, s_loads)

        @block.tensor
        def _(pe):
            pe.wait_ge(s["loaded"], 16 * s_loads)
            nc.tensor.matmul(m.psum[0][:, 0:1], wu, m.u0[:, :], start=True, stop=True).then_inc(s["u_done"], 1)


def sum_copies(nc, m):
    with ExitStack() as ctx:
        s = sems(nc, "added", "added_pool")
        came = ring(nc, "came", REP)
        size = NB * RW
        places = [m.both[:, 0:size], m.both[:, size:2 * size], m.work[:, 0:size]]
        cut = NB * 2 // 3 * RW
        block = ctx.enter_context(nc.Block())
        where = lambda r: places[0] if r == 0 else places[1 + (r - 1) % 2]

        @block.sync
        def _(sp):
            for r in range(REP):
                if r >= 3:
                    sp.wait_ge(s["added"], r - 2)
                    sp.wait_ge(s["added_pool"], r - 2)
                sp.dma_start(where(r), m.acc[r][0:NP, :].rearrange("(p b) f -> p (b f)", p=P)).then_inc(came[r], 16)

        def add(engine, ops, done, lo, hi):
            engine.wait_ge(came[0], 16)
            for r in range(1, REP):
                engine.wait_ge(came[r], 16)
                if r > 1:
                    engine.wait_ge(done, r - 1)
                to = places[0][:, lo:hi]
                ops.tensor_tensor(to, to, where(r)[:, lo:hi], ALU.add).then_inc(done, 1)

        @block.vector
        def _(dve):
            add(dve, nc.vector, s["added"], 0, cut)

        @block.gpsimd
        def _(pool):
            add(pool, nc.gpsimd, s["added_pool"], cut, size)


def columns_of(nc, m, terms, to, func=ACT.Copy, bias=None):
    T = len(terms)
    assert T <= 2
    units = GROUPS * T
    with ExitStack() as ctx:
        s = sems(nc, "brought", "turned", "columns", "product", "put")
        block = ctx.enter_context(nc.Block())

        def place(i, n):
            return (2 * i + n, 2 * i + n, 0) if T == 1 else (2 * i + n, i + n // 2, n % 2)

        out_bank = lambda n: 4 + (n * 2 if T == 1 else 0)

        @block.gpsimd
        def _(pool):
            def body(i, n):
                u, g, t = place(i, n)
                pool.wait_ge(s["turned"], two_before(u))
                settle(pool)
                bring(nc, pool, terms[t][0], g, m.together[n]).then_inc(s["brought"], 1)

            pool.sem_inc(s["turned"], 4)
            in_pairs(pool, units, body)

        @block.tensor
        def _(pe):
            def turn(i, n):
                u, g, t = place(i, n)
                pe.wait_ge(s["columns"], two_before(u))
                pe.wait_ge(s["brought"], u + 1)
                for b, (lo, hi) in enumerate(BANKS):
                    for q in range(lo, hi):
                        last = nc.tensor.transpose(m.psum[n % 2 * 2 + b][:, (q - lo) * P:(q - lo + 1) * P],
                                                   m.together[n % 2][:, q * P:(q + 1) * P], m.ident[:, :])
                    last.then_inc(s["turned"], 1)

            def multiply(i, n):
                u, g, t = place(i, n)
                if terms[t][1] is None:
                    return
                if t == 0:
                    pe.wait_ge(s["put"], two_before(g) if T == 1 else after(g))
                for b, (lo, hi) in enumerate(BANKS):
                    pe.wait_ge(s["columns"], after(u, b + 1))
                    nc.tensor.matmul(m.psum[out_bank(n) + b][:, 0:(hi - lo) * P], terms[t][1][:, :],
                                     m.turned[n][:, lo * P:hi * P], start=t == 0, stop=t == T - 1).then_inc(s["product"], 1)

            pe.sem_inc(s["columns"], 4)
            pe.sem_inc(s["put"], 4)
            in_pairs(pe, units, multiply, lead=turn)

        @block.scalar
        def _(act):
            a = nc.scalar
            kw = {} if bias is None else {"bias": bias[:, :]}
            part = lambda g, lo, hi: to[:, bass.ds(g * (GP * P) + lo * P, (hi - lo) * P)]

            def copy(i, n):
                u, g, t = place(i, n)
                if terms[t][1] is not None:
                    act.wait_ge(s["product"], two_before(u))
                for b, (lo, hi) in enumerate(BANKS):
                    act.wait_ge(s["turned"], after(u, b + 1))
                    if terms[t][1] is None:
                        settle(act)
                    a.activation(part(g, lo, hi) if terms[t][1] is None else m.turned[n % 2][:, lo * P:hi * P],
                                 m.psum[n % 2 * 2 + b][:, 0:(hi - lo) * P], ACT.Copy).then_inc(s["columns"], 1)

            def finish(i, n):
                u, g, t = place(i, n)
                if terms[t][1] is None or t < T - 1:
                    return
                for b, (lo, hi) in enumerate(BANKS):
                    act.wait_ge(s["product"], after(u, b + 1))
                    settle(act)
                    a.activation(part(g, lo, hi), m.psum[out_bank(n) + b][:, 0:(hi - lo) * P], func, **kw).then_inc(s["put"], 1)

            act.sem_inc(s["product"], 4)
            in_pairs(act, units, finish, lead=copy)


def product_of_columns(nc, m, frm, weight, to, bias=None):
    with ExitStack() as ctx:
        s = sems(nc, "product", "put")
        block = ctx.enter_context(nc.Block())

        @block.tensor
        def _(pe):
            def body(i, n):
                g = 2 * i + n
                pe.wait_ge(s["put"], two_before(g))
                for b, (lo, hi) in enumerate(BANKS):
                    nc.tensor.matmul(m.psum[n * 2 + b][:, 0:(hi - lo) * P], weight[:, :],
                                     frm[:, bass.ds(g * (GP * P) + lo * P, (hi - lo) * P)],
                                     start=True, stop=True).then_inc(s["product"], 1)

            pe.sem_inc(s["put"], 4)
            in_pairs(pe, GROUPS, body)

        @block.scalar
        def _(act):
            kw = {} if bias is None else {"bias": bias[:, :]}

            def body(i, n):
                g = 2 * i + n
                for b, (lo, hi) in enumerate(BANKS):
                    act.wait_ge(s["product"], g * 2 + b + 1)
                    settle(act)
                    nc.scalar.activation(to[:, bass.ds(g * (GP * P) + lo * P, (hi - lo) * P)],
                                         m.psum[n * 2 + b][:, 0:(hi - lo) * P],
                                         ACT.Copy if bias is None else ACT.Identity, **kw).then_inc(s["put"], 1)

            in_pairs(act, GROUPS, body)


def add_columns(nc, m, frm):
    with ExitStack() as ctx:
        s = sems(nc, "brought", "turned", "put")
        block = ctx.enter_context(nc.Block())

        @block.gpsimd
        def _(pool):
            def body(i, n):
                g = 2 * i + n
                pool.wait_ge(s["turned"], two_before(g))
                settle(pool)
                nc.gpsimd.tensor_copy(m.together[n], frm[:, bass.ds(g * (GP * P), GP * P)]).then_inc(s["brought"], 1)

            pool.sem_inc(s["turned"], 4)
            in_pairs(pool, GROUPS, body)

        @block.tensor
        def _(pe):
            def body(i, n):
                g = 2 * i + n
                pe.wait_ge(s["put"], two_before(g))
                pe.wait_ge(s["brought"], g + 1)
                for b, (lo, hi) in enumerate(BANKS):
                    for q in range(lo, hi):
                        last = nc.tensor.transpose(m.psum[n * 2 + b][:, (q - lo) * P:(q - lo + 1) * P],
                                                   m.together[n][:, q * P:(q + 1) * P], m.ident[:, :])
                    last.then_inc(s["turned"], 1)

            pe.sem_inc(s["put"], 4)
            in_pairs(pe, GROUPS, body)

        @block.vector
        def _(dve):
            def body(i, n):
                g = 2 * i + n
                for b, (lo, hi) in enumerate(BANKS):
                    dve.wait_ge(s["turned"], after(g, b + 1))
                    x = group_of(m.x, g, lo, hi)
                    nc.vector.tensor_tensor(x, x, m.psum[n * 2 + b][:, 0:(hi - lo) * P].rearrange("p (b f) -> p b f", f=D),
                                            ALU.add).then_inc(s["put"], 1)

            in_pairs(dve, GROUPS, body)


def batch_norm(nc, m, t, gamma, beta, func):
    with ExitStack() as ctx:
        s = sems(nc, "stats", "step", "folded", "rooted")
        whole, rest = divmod(Q * P, 512)
        chunks = whole + 1
        stats, mv = m.small[:, 0:chunks * 6], m.small[:, 6 * chunks:6 * chunks + 2]
        c = [m.small[:, 6 * chunks + 2 + i:6 * chunks + 3 + i] for i in range(5)]
        block = ctx.enter_context(nc.Block())

        @block.vector
        def _(dve):
            v = nc.vector
            for n in range(whole):
                v.bn_stats(stats[:, 6 * n:6 * n + 6], t[:, n * 512:(n + 1) * 512]).then_inc(s["stats"], 1)
            v.bn_stats(stats[0:D, 6 * whole:6 * chunks], t[0:D, whole * 512:Q * P]).then_inc(s["stats"], 1)
            v.bn_stats(stats[D:P, 6 * whole:6 * chunks], t[D:P, whole * 512:(Q - 1) * P + LAST]).then_inc(s["stats"], 1)
            dve.wait_ge(s["stats"], whole + 2)
            v.bn_aggr(mv, stats).then_inc(s["step"], 1)
            dve.wait_ge(s["step"], 1)
            v.tensor_tensor(c[0], mv[:, 0:1], m.share[:, :], ALU.mult).then_inc(s["step"], 1)
            dve.wait_ge(s["folded"], 1)
            v.tensor_copy(c[1], m.psum[0][:, 0:1]).then_inc(s["step"], 1)
            dve.wait_ge(s["step"], 3)
            v.tensor_tensor(c[2], mv[:, 0:1], c[1], ALU.subtract).then_inc(s["step"], 1)
            dve.wait_ge(s["step"], 4)
            v.tensor_tensor(c[2], c[2], c[2], ALU.mult).then_inc(s["step"], 1)
            dve.wait_ge(s["step"], 5)
            v.tensor_tensor(c[2], c[2], mv[:, 1:2], ALU.add).then_inc(s["step"], 1)
            dve.wait_ge(s["step"], 6)
            v.tensor_tensor(c[0], c[2], m.share[:, :], ALU.mult).then_inc(s["step"], 1)
            dve.wait_ge(s["folded"], 2)
            v.tensor_scalar(c[3], m.psum[1][:, 0:1], EPS, None, ALU.add).then_inc(s["step"], 1)
            dve.wait_ge(s["rooted"], 1)
            v.reciprocal(c[3], c[4]).then_inc(s["step"], 1)
            dve.wait_ge(s["step"], 9)
            v.tensor_tensor(m.col["scale"][:, :], c[3], gamma[:, :], ALU.mult).then_inc(s["step"], 1)
            dve.wait_ge(s["step"], 10)
            v.tensor_tensor(c[2], c[1], m.col["scale"][:, :], ALU.mult).then_inc(s["step"], 1)
            dve.wait_ge(s["step"], 11)
            v.tensor_tensor(m.col["shift"][:, :], beta[:, :], c[2], ALU.subtract).then_inc(s["step"], 1)

        @block.tensor
        def _(pe):
            for n, at in enumerate((2, 7)):
                pe.wait_ge(s["step"], at)
                nc.tensor.matmul(m.psum[n][:, 0:1], m.fold[:, :], c[0], start=True, stop=True).then_inc(s["folded"], 1)

        @block.scalar
        def _(act):
            act.wait_ge(s["step"], 8)
            nc.scalar.activation(c[4], c[3], ACT.Sqrt).then_inc(s["rooted"], 1)
            act.wait_ge(s["step"], 12)
            nc.scalar.activation(t[:, 0:Q * P], t[:, 0:Q * P], func, bias=m.col["shift"][:, :],
                                 scale=m.col["scale"][:, :])


def scale_by_degree_out(nc, m):
    with ExitStack() as ctx:
        s = sems(nc, "step", "rooted")
        block = ctx.enter_context(nc.Block())

        @block.vector
        def _(dve):
            v = nc.vector
            v.tensor_scalar(m.stat[:, :], m.dout[:, :], 1.0, None, ALU.max).then_inc(s["step"], 1)
            dve.wait_ge(s["rooted"], 1)
            v.reciprocal(m.stat[:, :], m.stat2[:, :]).then_inc(s["step"], 1)
            dve.wait_ge(s["step"], 2)
            h = m.h[:, :, 0:D]
            v.tensor_tensor(h, h, m.stat[:, :].unsqueeze(2).to_broadcast([P, NB, D]), ALU.mult)

        @block.scalar
        def _(act):
            act.wait_ge(s["step"], 1)
            nc.scalar.activation(m.stat2[:, :], m.stat[:, :], ACT.Sqrt).then_inc(s["rooted"], 1)


def keep_table(nc, m, rows):
    with ExitStack() as ctx:
        s = sems(nc, "kept")
        block = ctx.enter_context(nc.Block())

        @block.sync
        def _(sp):
            sp.dma_start(m.table.rearrange("(p b) f -> p b f", p=P), rows).then_inc(s["kept"], 16)
            sp.wait_ge(s["kept"], 16)


def finish_second_layer(nc, m):
    with ExitStack() as ctx:
        s = sems(nc, "step", "rooted")
        block = ctx.enter_context(nc.Block())
        work = m.work[:, 0:NB * D].rearrange("p (b f) -> p b f", b=NB)

        @block.vector
        def _(dve):
            v = nc.vector
            v.tensor_copy(m.din[:, :].unsqueeze(2), m.pair[:, :, D:RW]).then_inc(s["step"], 1)
            dve.wait_ge(s["step"], 1)
            v.tensor_scalar(m.stat[:, :], m.din[:, :], 1.0, None, ALU.max).then_inc(s["step"], 1)
            dve.wait_ge(s["rooted"], 1)
            v.reciprocal(m.stat[:, :], m.stat2[:, :]).then_inc(s["step"], 1)
            dve.wait_ge(s["step"], 3)
            v.tensor_tensor(work, m.pair[:, :, 0:D], m.stat[:, :].unsqueeze(2).to_broadcast([P, NB, D]),
                            ALU.mult).then_inc(s["step"], 1)
            v.tensor_tensor(m.x[:, :, :], m.x[:, :, :], m.row["l1_bias"][:, :].unsqueeze(1).to_broadcast([P, NB, D]),
                            ALU.add).then_inc(s["step"], 1)
            dve.wait_ge(s["step"], 5)
            v.tensor_tensor(m.x[:, :, :], m.x[:, :, :], work, ALU.add)

        @block.scalar
        def _(act):
            act.wait_ge(s["step"], 2)
            nc.scalar.activation(m.stat2[:, :], m.stat[:, :], ACT.Sqrt).then_inc(s["rooted"], 1)


def norm_rows(nc, dve, m, s, first, mean, square, count):
    v = nc.vector
    mu, var, tmp = (m.small[:, i * D:(i + 1) * D] for i in range(3))
    n = first

    def link(ins):
        nonlocal n
        ins.then_inc(s["step"], 1)
        n += 1
        dve.wait_ge(s["step"], n)

    link(v.tensor_scalar(mu, mean, 1.0 / count, None, ALU.mult))
    link(v.tensor_tensor(tmp, mu, mu, ALU.mult))
    link(v.tensor_scalar(var, square, 1.0 / count, None, ALU.mult))
    link(v.tensor_tensor(var, var, tmp, ALU.subtract))
    link(v.tensor_scalar(var, var, 0.0, EPS, ALU.max, ALU.add))
    return n, mu, var, tmp, link


def rows_of_norm(nc, dve, s, m, gamma, beta, mu, var, tmp, link):
    v = nc.vector
    link(v.reciprocal(tmp, m.small[:, 3 * D:4 * D]))
    link(v.tensor_tensor(m.scale_row[:, 0:D], tmp, gamma[:, :], ALU.mult))
    link(v.tensor_copy(m.scale_row[:, D:P], m.scale_row[:, 0:D]))
    link(v.tensor_tensor(tmp, mu, m.scale_row[:, 0:D], ALU.mult))
    link(v.tensor_tensor(m.shift_row[:, 0:D], beta[:, :], tmp, ALU.subtract))
    link(v.tensor_copy(m.shift_row[:, D:P], m.shift_row[:, 0:D]))


def norm_of_edge_input(nc, m):
    with ExitStack() as ctx:
        s = sems(nc, "step", "ready", "brought", "group", "sums", "kept", "turned", "scaled", "formed",
                 "squares", "products", "rooted")
        block = ctx.enter_context(nc.Block())
        left = m.pair[:, :, 0:D]
        sums = m.work[0:RW, 0:P]
        wide_sum = m.work[:, P:2 * P]
        prod, prod_ea = m.work[0:D, 2 * P:2 * P + D], m.work[0:D, 2 * P + D:3 * P]

        @block.vector
        def _(dve):
            v = nc.vector
            v.memset(m.h[:, :, D:RW], 1.0).then_inc(s["ready"], 1)
            dve.wait_ge(s["ready"], 2)
            v.tensor_scalar(m.h[:, NB - 1, :], m.h[:, NB - 1, :], m.valid[:, :], None, ALU.mult).then_inc(s["ready"], 1)
            dve.wait_ge(s["ready"], 3)
            v.tensor_tensor(left, m.h[:, :, 0:D], m.din[:, :].unsqueeze(2).to_broadcast([P, NB, D]),
                            ALU.mult).then_inc(s["ready"], 1)
            dve.wait_ge(s["sums"], 1)
            v.tensor_copy(sums, m.psum[0][0:RW, 0:P]).then_inc(s["kept"], 1)
            dve.wait_ge(s["turned"], 1)
            v.tensor_scalar(m.turned_gram[:, 0:D], m.psum[1][:, 0:D], m.twice[:, :], None, ALU.mult).then_inc(s["scaled"], 1)
            v.tensor_copy(m.turned_gram[:, D:RW], m.psum[1][:, D:RW]).then_inc(s["scaled"], 1)
            dve.wait_ge(s["scaled"], 2)
            v.tensor_scalar(wide_sum, m.ones[:, :], m.turned_gram[:, D:RW], None, ALU.mult).then_inc(s["scaled"], 1)
            dve.wait_ge(s["formed"], 1)
            v.tensor_tensor(prod, m.psum[2][0:D, 0:D], m.w1a[0:D, :], ALU.mult).then_inc(s["squares"], 1)
            dve.wait_ge(s["formed"], 2)
            v.tensor_tensor(prod_ea, m.psum[3][0:D, 0:D], m.w1a_ea[:, :], ALU.mult).then_inc(s["squares"], 1)
            dve.wait_ge(s["products"], 2)
            n, mu, var, tmp, link = norm_rows(nc, dve, m, s, 0, m.psum[4][:, 0:D], m.psum[5][:, 0:D], E)
            dve.wait_ge(s["rooted"], 1)
            rows_of_norm(nc, dve, s, m, m.row["g1a"], m.row["b1a"], mu, var, tmp, link)
            v.tensor_tensor(m.w["l3_h"][:, :], m.w["l3_h"][:, :], m.scale_row[:, :], ALU.mult)

        @block.gpsimd
        def _(pool):
            nc.gpsimd.affine_select(out=m.valid[:, :], in_=m.valid[:, :], compare_op=ALU.is_gt, fill=0.0,
                                    base=LAST, pattern=[[0, 1]], channel_multiplier=-1).then_inc(s["ready"], 1)
            pool.wait_ge(s["ready"], 4)
            pool.sem_inc(s["group"], 2)

            def body(i, n):
                g = 2 * i + n
                pool.wait_ge(s["group"], g + 1)
                settle(pool)
                nc.gpsimd.tensor_copy(m.counted[n].rearrange("p (b f) -> p b f", f=RW),
                                      group_of(m.h, g, width=RW)).then_inc(s["brought"], 1)

            in_pairs(pool, GROUPS, body)

        @block.tensor
        def _(pe):
            nc.tensor.matmul(m.psum[0][0:RW, 0:P], m.zero[:, 0:RW], m.ones[:, :], start=True, stop=False,
                             skip_group_check=True)
            pe.wait_ge(s["ready"], 4)

            def body(i, n):
                g = 2 * i + n
                pe.wait_ge(s["brought"], g + 1)
                for b in range(2 * GP):
                    last = nc.tensor.matmul(m.psum[0][0:RW, 0:P], m.counted[n][:, b * RW:(b + 1) * RW],
                                            m.both[:, bass.ds(g * (2 * GP * 2 * D) + b * 2 * D, 2 * D)],
                                            start=False, stop=False, skip_group_check=True)
                last.then_inc(s["group"], 1)

            in_pairs(pe, GROUPS, body)
            nc.tensor.matmul(m.psum[0][0:RW, 0:P], m.zero[:, 0:RW], m.ones[:, :], start=False, stop=True,
                             skip_group_check=True).then_inc(s["sums"], 1)
            pe.wait_ge(s["kept"], 1)
            nc.tensor.transpose(m.psum[1][:, 0:RW], sums, m.ident[0:RW, 0:RW]).then_inc(s["turned"], 1)
            pe.wait_ge(s["scaled"], 3)
            nc.tensor.matmul(m.psum[2][0:D, 0:D], m.turned_gram[:, 0:D], m.w1a[:, :], start=True, stop=True).then_inc(s["formed"], 1)
            nc.tensor.matmul(m.psum[3][0:D, 0:D], m.gram[:, 0:D], m.w1a_ea[:, :], start=True, stop=True).then_inc(s["formed"], 1)
            nc.tensor.matmul(m.psum[4][:, 0:D], wide_sum, m.w1a[:, :], start=True, stop=True).then_inc(s["products"], 1)
            pe.wait_ge(s["squares"], 2)
            nc.tensor.matmul(m.psum[5][:, 0:D], m.ones[0:D, :], prod, start=True, stop=False)
            nc.tensor.matmul(m.psum[5][:, 0:D], m.ones[0:D, :], prod_ea, start=False, stop=True).then_inc(s["products"], 1)

        @block.scalar
        def _(act):
            act.wait_ge(s["step"], 5)
            nc.scalar.activation(m.small[:, 3 * D:4 * D], m.small[:, D:2 * D], ACT.Sqrt).then_inc(s["rooted"], 1)


def norm_of_edge_output(nc, m):
    with ExitStack() as ctx:
        s = sems(nc, "step", "widened", "formed", "squares", "products", "rooted", "mean")
        block = ctx.enter_context(nc.Block())
        w = m.w["l3_b"]
        wide_sum, prod = m.work[0:D, 0:P], m.work[0:D, P:P + D]

        @block.vector
        def _(dve):
            v = nc.vector
            v.tensor_scalar(wide_sum, m.ones[0:D, :], m.gram[:, D:RW], None, ALU.mult).then_inc(s["widened"], 1)
            dve.wait_ge(s["formed"], 1)
            v.tensor_tensor(prod, m.psum[0][0:D, 0:D], w[0:D, 0:D], ALU.mult).then_inc(s["squares"], 1)
            dve.wait_ge(s["products"], 2)
            n, mu, var, tmp, link = norm_rows(nc, dve, m, s, 0, m.psum[1][:, 0:D], m.psum[2][:, 0:D], E)
            dve.wait_ge(s["rooted"], 1)
            rows_of_norm(nc, dve, s, m, m.row["g1b"], m.row["b1b"], mu, var, tmp, link)
            v.tensor_tensor(w[:, :], w[:, :], m.scale_row[:, :], ALU.mult)
            v.tensor_scalar(m.stat[:, :], m.dout[:, :], 1.0, None, ALU.max).then_inc(s["mean"], 1)
            dve.wait_ge(s["mean"], 1)
            v.reciprocal(m.stat2[:, :], m.stat[:, :]).then_inc(s["mean"], 1)
            dve.wait_ge(s["mean"], 2)
            sums = m.both[:, 0:NB * RW].rearrange("p (b f) -> p b f", f=RW)[:, :, 0:D]
            v.tensor_tensor(sums, sums, m.stat2[:, :].unsqueeze(2).to_broadcast([P, NB, D]), ALU.mult)
            v.tensor_scalar(m.din[:, :], m.dout[:, :], 1.0, None, ALU.min)

        @block.tensor
        def _(pe):
            nc.tensor.matmul(m.psum[0][0:D, 0:D], m.gram[:, 0:D], w[0:D, 0:D], start=True, stop=True).then_inc(s["formed"], 1)
            pe.wait_ge(s["widened"], 1)
            nc.tensor.matmul(m.psum[1][:, 0:D], wide_sum, w[0:D, 0:D], start=True, stop=True).then_inc(s["products"], 1)
            pe.wait_ge(s["squares"], 1)
            nc.tensor.matmul(m.psum[2][:, 0:D], m.ones[0:D, :], prod, start=True, stop=True).then_inc(s["products"], 1)

        @block.scalar
        def _(act):
            act.wait_ge(s["step"], 5)
            nc.scalar.activation(m.small[:, 3 * D:4 * D], m.small[:, D:2 * D], ACT.Sqrt).then_inc(s["rooted"], 1)


def keep_degree_out(nc, m):
    with ExitStack() as ctx:
        block = ctx.enter_context(nc.Block())

        @block.vector
        def _(dve):
            sums = m.both[:, 0:NB * RW].rearrange("p (b f) -> p b f", f=RW)
            nc.vector.tensor_copy(m.dout[:, :].unsqueeze(2), sums[:, :, D:RW])


def store(nc, m, out):
    with ExitStack() as ctx:
        s = sems(nc, "stored")
        block = ctx.enter_context(nc.Block())

        @block.sync
        def _(sp):
            sp.dma_start(node_rows(out, 0, NB - 1), m.x[:, 0:NB - 1, :]).then_inc(s["stored"], 16)
            sp.dma_start(out[(NB - 1) * P:N, :], m.x[0:LAST, NB - 1, :]).then_inc(s["stored"], 16)
            sp.wait_ge(s["stored"], 32)


def gnn_stack(nc, a, out):
    with ExitStack() as ctx:
        m = allocate(nc, ctx)
        first = m.both[:, 0:NB * RW].rearrange("p (b f) -> p b f", f=RW)
        second = m.both[:, NB * RW:NB * RW + NB * D].rearrange("p (b f) -> p b f", f=D)
        work = m.work[:, 0:NB * D]
        columns_in_h = m.h[:, :, :].rearrange("p b f -> p (b f)")[:, 0:NB * D]

        with nc.cleanup_on_exit():
            m.cleared = nc.alloc_semaphore(name="cleared")
            constants(nc, m)
            load_parameters(nc, m, a)
            plan_steps(nc, m, a)

            layer_norm(nc, m)
            node_product(nc, m, [m.h], m.w["hamilton"], put_rows(nc, m.pair))
            steps_by_source(nc, m, last_layer=False)
            sum_copies(nc, m)
            keep_degree_out(nc, m)
            columns_of(nc, m, [([first], None)], work)
            batch_norm(nc, m, work, m.col["gamma"], m.col["beta"], ACT.Tanh)
            add_columns(nc, m, work)

        with nc.cleanup_on_exit():
            layer_norm(nc, m)
            scale_by_degree_out(nc, m)
            node_product(nc, m, [m.h], m.w["l1"], put_rows(nc, work.rearrange("p (b f) -> p b f", f=D)))
            keep_table(nc, m, work.rearrange("p (b f) -> p b f", f=D))
            steps_by_target(nc, m, a, with_attr=False)
            finish_second_layer(nc, m)

        with nc.cleanup_on_exit():
            layer_norm(nc, m)
            keep_table(nc, m, m.h[:, :, 0:D])
            steps_by_target(nc, m, a, with_attr=True)
            columns_of(nc, m, [([m.h, m.pair], m.w["l2a"])], work, ACT.Relu, m.col["l2_b1"])
            product_of_columns(nc, m, work, m.w["l2b"], columns_in_h, m.col["l2_b2"])
            add_columns(nc, m, columns_in_h)

        with nc.cleanup_on_exit():
            layer_norm(nc, m)
            norm_of_edge_input(nc, m)
            node_product(nc, m, [m.h], m.w["l3_h"], put_rows(nc, m.pair), row=m.shift_row)
            steps_by_source(nc, m, last_layer=True)
            sum_copies(nc, m)
            norm_of_edge_output(nc, m)
            has_edge = lambda g, lo, hi: m.din[:, bass.ds(g * (2 * GP) + 2 * lo, 2 * (hi - lo))].unsqueeze(2)\
                .to_broadcast([P, 2 * (hi - lo), D])
            node_product(nc, m, [first], m.w["l3_b"],
                         lambda g, lo, hi, rows: nc.vector.tensor_tensor(group_of(second, g, lo, hi), rows, has_edge(g, lo, hi),
                                                                         ALU.mult), row=m.shift_row)
            columns_of(nc, m, [([m.h], m.w["l3_x"]), ([second], m.w["l3_agg"])], work, ACT.Identity, m.col["l3_u"])
            batch_norm(nc, m, work, m.col["g2a"], m.col["b2a"], ACT.Relu)
            product_of_columns(nc, m, work, m.w["l3_out"], columns_in_h)
            batch_norm(nc, m, columns_in_h, m.col["g2b"], m.col["b2b"], ACT.Identity)
            add_columns(nc, m, columns_in_h)
            store(nc, m, out)


_SHAPE = (N, D)


def kernel(**inputs):
    import numpy as np
    import concourse.bacc as bacc
    from concourse.bass_utils import run_bass_kernel_spmd

    nc = bacc.Bacc("TRN2", target_bir_lowering=False, num_devices=1)
    arrays = {}
    given = {}

    def give(name, array):
        array = np.ascontiguousarray(array)
        arrays[f"in_{name}"] = array
        given[name] = nc.dram_tensor(f"in_{name}", array.shape, mybir.dt.from_np(array.dtype), kind="ExternalInput").ap()

    src, dst, edge_weight = (
        np.pad(np.asarray(inputs[name]), (0, EP - E), constant_values=fill).reshape(TC * P, P)
        for name, fill in (("src", PAD_SOURCE), ("dst", PAD_TARGET), ("edge_weight", 0)))
    give("ends", np.concatenate([src, dst], axis=1))
    give("edge_weight", edge_weight)
    attr = np.pad(np.asarray(inputs["edge_attr_64"]), ((0, NT * P - E), (0, 0)))
    give("edge_attr", attr)
    give("attr_turned", attr.reshape(NT, P, D).transpose(0, 2, 1).reshape(NT * D, P))
    names = {"x": "x",
             "gamma": "L0_gnn_gamma", "beta": "L0_gnn_beta", "l1_w": "L1_gnn_weight", "l1_bias": "L1_gnn_bias",
             "l2_w1": "L2_gnn_W1", "l2_b1": "L2_gnn_b1", "l2_w2": "L2_gnn_W2", "l2_b2": "L2_gnn_b2", "u": "L3_gnn_u",
             "w1a": "L3_gnn_W1a", "g1a": "L3_gnn_g1a", "b1a": "L3_gnn_b1a", "w1b": "L3_gnn_W1b", "g1b": "L3_gnn_g1b",
             "b1b": "L3_gnn_b1b", "w2a": "L3_gnn_W2a", "g2a": "L3_gnn_g2a", "b2a": "L3_gnn_b2a", "w2b": "L3_gnn_W2b",
             "g2b": "L3_gnn_g2b", "b2b": "L3_gnn_b2b"}
    for name, theirs in names.items():
        give(name, inputs[theirs])
    part = np.array([[0, 1, 2, 3], [1, 0, 3, 2], [2, 3, 0, 1], [3, 2, 1, 0]])
    sign = np.array([[1, -1, -1, -1], [1, 1, -1, 1], [1, 1, 1, -1], [1, -1, 1, 1]], np.float32)
    n = np.arange(D)
    place = np.empty(D, np.int64)
    place[n * 4 % D + n * 4 // D] = n
    row, col = np.meshgrid(place, place, indexing="ij")
    quarter = D // 4
    weight = np.asarray(inputs["L0_gnn_weight"])
    give("hamilton", weight[row % quarter, part[row // quarter, col // quarter] * quarter + col % quarter])
    give("signs", sign[row // quarter, col // quarter])
    out = nc.dram_tensor("out_0", _SHAPE, F32, kind="ExternalOutput").ap()
    gnn_stack(nc, given, out)
    r = run_bass_kernel_spmd(nc, [arrays], core_ids=[0])
    return r.results[0]["out_0"]
```
